# Optimizing a Trainium2 kernel written in Bass

```python
import numpy as np
import jax
import jax.numpy as jnp

def _softmax(x, axis=-1):
    return jax.nn.softmax(x, axis=axis)

def _gelu(x):
    return jax.nn.gelu(x, approximate=True)

def _silu(x):
    return jax.nn.silu(x)

def _sigmoid(x):
    return jax.nn.sigmoid(x)

def _layernorm(x, axis=-1, eps=1e-05):
    m = jnp.mean(x, axis=axis, keepdims=True)
    v = jnp.var(x, axis=axis, keepdims=True)
    return (x - m) / jnp.sqrt(v + eps)

def _scatter_add(tgt, idx, src, axis=0):
    return tgt.at[idx].add(src)

def _segment_sum(src, seg, n):
    return jax.ops.segment_sum(src, seg, n)
kernel_name = 'mk_vit_tower_postln_d1_tok_img768_r4_c92eb0'

def setup_inputs(seed: int=0):
    np.random.seed(seed)
    _w = jnp.asarray

    def _rec_inputs():
        import jax
        import jax.numpy as jnp
        _rk = jax.random.key(seed)
        x = -0.00016672 + 0.999947 * jax.random.normal(jax.random.fold_in(_rk, 1), (128, 3, 64, 64), jnp.float32)
        return x
    x = _rec_inputs()

    def _L0_tok_setup():
        import jax, jax.numpy as jnp
        import numpy as np
        P = 16
        EMBED_DIM = 192
        key = jax.random.key(seed)
        k1, k2 = jax.random.split(key)
        x = jax.random.normal(k1, (64, 3, 96, 96), dtype=jnp.float32)
        W = jax.random.normal(k2, (3 * P * P, EMBED_DIM), dtype=jnp.float32) * (1.0 / np.sqrt(3 * P * P))
        return {'x': x, 'W': W}
    _L0_tok_all = _L0_tok_setup()
    _L0_tok_in = {k: v for k, v in _L0_tok_all.items() if k in ('W',)}
    del _L0_tok_all

    def _L0_attn_setup():
        import jax, jax.numpy as jnp
        import numpy as np
        import math
        B, N, DIM = (4, 512, 192)
        HEADS, DIM_HEAD = (12, 64)
        SCALE = math.sqrt(DIM_HEAD)

        def _split_heads(t):
            b, n, _ = t.shape
            return t.reshape(b, n, HEADS, DIM_HEAD).transpose(0, 2, 1, 3)
        key = jax.random.key(seed)
        ks = jax.random.split(key, 5)
        inner = HEADS * DIM_HEAD
        x = jax.random.normal(ks[0], (B, N, DIM), dtype=jnp.float32)
        w_q = jax.random.normal(ks[1], (DIM, inner), dtype=jnp.float32) * 0.02
        w_k = jax.random.normal(ks[2], (DIM, inner), dtype=jnp.float32) * 0.02
        w_v = jax.random.normal(ks[3], (DIM, inner), dtype=jnp.float32) * 0.02
        w_o = jax.random.normal(ks[4], (inner, DIM), dtype=jnp.float32) * 0.02
        b_o = jnp.zeros((DIM,), dtype=jnp.float32)
        return {'x': x, 'w_q': w_q, 'w_k': w_k, 'w_v': w_v, 'w_o': w_o, 'b_o': b_o}
    _L0_attn_all = _L0_attn_setup()
    _L0_attn_in = {k: v for k, v in _L0_attn_all.items() if k in ('w_q', 'w_k', 'w_v', 'w_o', 'b_o')}
    del _L0_attn_all

    def _L0_ffn_setup():
        import jax, jax.numpy as jnp
        import numpy as np
        SEQ, BATCH, EMBED = (256, 2, 192)
        E = 16
        FFN_H = 384
        K_SHARED = 1
        K_ROUTE = 3
        LN_EPS = 1e-05
        NEG_INF = -1000000000.0
        key = jax.random.key(seed)
        ks = jax.random.split(key, 4)
        x = jax.random.normal(ks[0], (SEQ, BATCH, EMBED), dtype=jnp.float32)
        gate_w = jax.random.normal(ks[1], (EMBED, E), dtype=jnp.float32) * 0.02
        gate_b = jnp.zeros((E,), jnp.float32)
        fc1_w = jax.random.normal(ks[2], (E, EMBED, FFN_H), dtype=jnp.float32) * 0.02
        fc1_b = jnp.zeros((E, FFN_H), jnp.float32)
        ln_w = jnp.ones((E, FFN_H), jnp.float32)
        ln_b = jnp.zeros((E, FFN_H), jnp.float32)
        fc2_w = jax.random.normal(ks[3], (E, FFN_H, EMBED), dtype=jnp.float32) * 0.02
        fc2_b = jnp.zeros((E, EMBED), jnp.float32)
        return {'x': x, 'gate_w': gate_w, 'gate_b': gate_b, 'fc1_w': fc1_w, 'fc1_b': fc1_b, 'ln_w': ln_w, 'ln_b': ln_b, 'fc2_w': fc2_w, 'fc2_b': fc2_b}
    _L0_ffn_all = _L0_ffn_setup()
    _L0_ffn_in = {k: v for k, v in _L0_ffn_all.items() if k in ('gate_w', 'gate_b', 'fc1_w', 'fc1_b', 'ln_w', 'ln_b', 'fc2_w', 'fc2_b')}
    del _L0_ffn_all
    return {'x': x, 'L0_tok_W': _L0_tok_in['W'], 'L0_attn_w_q': _L0_attn_in['w_q'], 'L0_attn_w_k': _L0_attn_in['w_k'], 'L0_attn_w_v': _L0_attn_in['w_v'], 'L0_attn_w_o': _L0_attn_in['w_o'], 'L0_attn_b_o': _L0_attn_in['b_o'], 'L0_ffn_gate_w': _L0_ffn_in['gate_w'], 'L0_ffn_gate_b': _L0_ffn_in['gate_b'], 'L0_ffn_fc1_w': _L0_ffn_in['fc1_w'], 'L0_ffn_fc1_b': _L0_ffn_in['fc1_b'], 'L0_ffn_ln_w': _L0_ffn_in['ln_w'], 'L0_ffn_ln_b': _L0_ffn_in['ln_b'], 'L0_ffn_fc2_w': _L0_ffn_in['fc2_w'], 'L0_ffn_fc2_b': _L0_ffn_in['fc2_b']}

def reference(x, L0_tok_W, L0_attn_w_q, L0_attn_w_k, L0_attn_w_v, L0_attn_w_o, L0_attn_b_o, L0_ffn_gate_w, L0_ffn_gate_b, L0_ffn_fc1_w, L0_ffn_fc1_b, L0_ffn_ln_w, L0_ffn_ln_b, L0_ffn_fc2_w, L0_ffn_fc2_b):
    import jax
    import jax.numpy as jnp

    def _L0_tok_ref(x, W):
        import jax, jax.numpy as jnp
        import numpy as np
        P = 16
        EMBED_DIM = 192
        B, C, H, Wd = x.shape
        xp = x.reshape(B, C, H // P, P, Wd // P, P)
        xp = jnp.transpose(xp, (0, 2, 4, 3, 5, 1))
        xp = xp.reshape(B, H // P * (Wd // P), P * P * C)
        return jnp.einsum('bnd,de->bne', xp, W)

    def _L0_attn_ref(x, w_q, w_k, w_v, w_o, b_o):
        import jax, jax.numpy as jnp
        import numpy as np
        import math
        B, N, DIM = (4, 512, 192)
        HEADS, DIM_HEAD = (12, 64)
        SCALE = math.sqrt(DIM_HEAD)

        def _split_heads(t):
            b, n, _ = t.shape
            return t.reshape(b, n, HEADS, DIM_HEAD).transpose(0, 2, 1, 3)
        q = _split_heads(x @ w_q)
        k = _split_heads(x @ w_k)
        v = _split_heads(x @ w_v)
        scores = jnp.einsum('bhnd,bhmd->bhnm', q, k) / SCALE
        attn = jax.nn.softmax(scores, axis=-1)
        h = jnp.einsum('bhnm,bhmd->bhnd', attn, v)
        H = h.transpose(0, 2, 1, 3).reshape(x.shape[0], x.shape[1], HEADS * DIM_HEAD)
        out = H @ w_o + b_o
        return out

    def _L0_ffn_ref(x, gate_w, gate_b, fc1_w, fc1_b, ln_w, ln_b, fc2_w, fc2_b):
        import jax, jax.numpy as jnp
        import numpy as np
        SEQ, BATCH, EMBED = (256, 2, 192)
        E = 16
        FFN_H = 384
        K_SHARED = 1
        K_ROUTE = 3
        LN_EPS = 1e-05
        NEG_INF = -1000000000.0
        S, B, D = x.shape
        T = S * B
        xf = x.reshape(T, D)
        scores = xf @ gate_w + gate_b
        scores = scores.at[:, :K_SHARED].set(NEG_INF)
        probs = jax.nn.softmax(scores, axis=-1)
        topv, topi = jax.lax.top_k(probs, K_ROUTE)
        combine = jnp.zeros((T, E), xf.dtype)
        combine = combine.at[jnp.arange(T)[:, None], topi].add(topv)
        combine = combine.at[:, :K_SHARED].add(1.0)
        h = jnp.einsum('td,edh->eth', xf, fc1_w) + fc1_b[:, None, :]
        h = jax.nn.gelu(h, approximate=False)
        mu = h.mean(-1, keepdims=True)
        var = h.var(-1, keepdims=True)
        h = (h - mu) * jax.lax.rsqrt(var + LN_EPS) * ln_w[:, None, :] + ln_b[:, None, :]
        y = jnp.einsum('eth,ehd->etd', h, fc2_w) + fc2_b[:, None, :]
        out = jnp.einsum('te,etd->td', combine, y)
        return out.reshape(S, B, D)
    h = _L0_tok_ref(x, L0_tok_W)
    h = _layernorm(h + _L0_attn_ref(h, L0_attn_w_q, L0_attn_w_k, L0_attn_w_v, L0_attn_w_o, L0_attn_b_o), axis=-1)
    h = _layernorm(h + _L0_ffn_ref(h, L0_ffn_gate_w, L0_ffn_gate_b, L0_ffn_fc1_w, L0_ffn_fc1_b, L0_ffn_ln_w, L0_ffn_ln_b, L0_ffn_fc2_w, L0_ffn_fc2_b), axis=-1)
    return h

_drawn_inputs = setup_inputs


def setup_inputs(seed=0):
    import zlib

    import numpy as np

    out = dict(_drawn_inputs(seed))
    spreads = {'L0_attn_b_o': (0.0, 0.1),
     'L0_ffn_gate_b': (0.0, 0.1),
     'L0_ffn_fc1_b': (0.0, 0.1),
     'L0_ffn_ln_w': (1.0, 0.2),
     'L0_ffn_ln_b': (0.0, 0.1),
     'L0_ffn_fc2_b': (0.0, 0.1)}
    factors = {'L0_attn_w_q': 8.0, 'L0_attn_w_k': 8.0}
    for name, (base, spread) in spreads.items():
        noise = np.random.default_rng([zlib.crc32(name.encode()), seed]).standard_normal(out[name].shape)
        drawn = base * np.exp(spread * noise) if base else spread * noise
        out[name] = jnp.asarray(drawn.astype(out[name].dtype))
    for name, factor in factors.items():
        out[name] = (out[name] * factor).astype(out[name].dtype)
    return out
```

```python
from contextlib import ExitStack

import concourse.bass as bass
from concourse import mybir

F32 = mybir.dt.float32
F32R = mybir.dt.float32r
ALU = mybir.AluOpType
ACT = mybir.ActivationFunctionType
AX = mybir.AxisListType

P = 128
H = 64
PATCH = 16
IMAGES, CHANNELS, SIDE = 128, 3, 64
SEQ = (SIDE // PATCH) ** 2
TOK = IMAGES * SEQ
NT = TOK // P
KC = CHANNELS * PATCH * PATCH // P
D = 192
DB = D - P
HEADS, DH = 12, 64
INNER = HEADS * DH
IC = INNER // P
SCALE = 1.0 / 8.0
MASKED = -1e30
E = 16
F = 384
FC = F // P
SHARED, ROUTE = 1, 3
NEG_INF = -1e9
EPS = 1e-5

GT = 2
GTOK = GT * P
NG = NT // GT
ST = 4
STOK = ST * P
NQ = NT // ST
STEPS = E * NQ
YW = 256
CW = D + 2
SUMG, SUMSQ = D, D + 2
ITEMS = 2 * FC + 2 * GT
NQK = 2 * IC // 2
EVACS = IC // 2 + 2 * (IC // 2) + 2 * GT

C_ID, C_MASK, C_ONES, C_EYE, C_ROW, C_HALF, C_END = 0, 128, 160, 288, 432, 440, 456


def need(eng, sem, count):
    if not (isinstance(count, int) and count <= 0):
        eng.wait_ge(sem, count)


def held(eng, sem, count):
    need(eng, sem, count)
    eng.nop(nofuse=True)


def pairs(eng, n, body):
    for k in (0, 1):
        body(k, k)
    with eng.Fori(1, n // 2 - 1) as turn:
        for k in (0, 1):
            body(turn * 2 + k, k)
    for k in (n - 2, n - 1):
        body(k, k % 2)


def stack_terms(w, xh, xl):
    return [(w[:, 0, :], xh[:, 0, :]), (w[:, 0, :], xl[:, 0, :]), (w[:, 1, :], xh[:, 0, :]),
            (w[:, 2, :], xh[:, 1, :]), (w[:, 3, :], xl[:, 1, :])]


def pack_high(dve, w, raw):
    dve.tensor_copy(w[:, 0, :], raw[:, 0, :])
    dve.tensor_copy(w[0:H, 2, :], raw[0:H, 1, :])
    return dve.tensor_copy(w[H:P, 3, :], raw[H:P, 1, :])


def pack_low(dve, w, raw):
    dve.tensor_tensor(w[:, 1, :], raw[:, 0, :], w[:, 0, :].bitcast(F32), ALU.subtract)
    dve.tensor_tensor(w[H:P, 2, :], raw[H:P, 1, :], w[H:P, 3, :].bitcast(F32), ALU.subtract)
    return dve.tensor_tensor(w[0:H, 3, :], raw[0:H, 1, :], w[0:H, 2, :].bitcast(F32), ALU.subtract)


def attention(nc, ins, consts, gate_pack, XH, XL, acc):
    with ExitStack() as ctx:
        def sb(name, shape, dt=F32):
            return ctx.enter_context(nc.sbuf_tensor(name, shape, dt))

        def ps(name, shape):
            return ctx.enter_context(nc.psum_tensor(name, shape, F32))

        def sem(name):
            return ctx.enter_context(nc.semaphore(name))

        xin = [sb(f"xin{b}", [P, GT, KC, P]) for b in range(2)]
        tokw = sb("tokw", [P, KC, D])
        wraw = sb("wraw", [P, 2, INNER])
        graw = sb("graw", [P, 2, E])
        wqkv = sb("wqkv", [P, 4, 3 * INNER], F32R)
        wo = sb("wo", [P, IC, D])
        bo = sb("bo", [P, D])
        h0row = sb("h0row", [P, GT, D + DB])
        h0hi = [sb(f"h0hi{b}", [P, 2, GTOK], F32R) for b in range(2)]
        h0lo = [sb(f"h0lo{b}", [P, 2, GTOK], F32R) for b in range(2)]
        qT = [sb(f"qT{b}", [P, IC, GTOK]) for b in range(2)]
        kT = [sb(f"kT{b}", [P, IC, 2, GTOK]) for b in range(2)]
        v = [sb(f"v{b}", [P, GT, INNER]) for b in range(2)]
        scores = sb("scores", [P, HEADS, 32])
        probs = sb("probs", [P, HEADS, 32])
        smax = sb("smax", [P, HEADS])
        ssum = sb("ssum", [P, HEADS])
        srec = sb("srec", [P, HEADS])
        pT = [sb(f"pT{t}", [P, HEADS, P]) for t in range(GT)]
        oT = [sb(f"oT{t}", [P, IC, P]) for t in range(GT)]
        z = [sb(f"z{t}", [P, D]) for t in range(GT)]
        stats = sb("stats", [P, GT, 6])
        meanvar = sb("meanvar", [P, GT, 2])
        vareps = sb("vareps", [P, GT])
        rstd = sb("rstd", [P, GT])
        x1row = sb("x1row", [P, GT, D + DB])

        p_row = ps("p_row", [P, 512])
        p_qkv = [ps(f"p_qkv{j}", [P, 512]) for j in range(2)]
        p_sc = ps("p_sc", [P, HEADS, P])
        p_o = ps("p_o", [P, 1024])

        ident = consts[:, C_ID:C_ID + P]
        mask = consts[:, C_MASK:C_MASK + 32]
        half = consts[:, C_HALF:C_HALF + GT]

        s_const = sem("s_const")
        s_x = [sem(f"s_patches{b}") for b in range(2)]
        s_tokw = sem("s_tokw")
        s_wraw = sem("s_wraw")
        s_graw = sem("s_graw")
        s_wo = sem("s_wo")
        s_bo = sem("s_bo")
        s_packh = sem("s_packh")
        s_packl = sem("s_packl")
        s_zero = sem("s_zero")
        s_e = sem("s_e")
        s_row = sem("s_row")
        s_res = sem("s_res")
        s_t0 = sem("s_t0")
        s_hi0 = sem("s_hi0")
        s_lo0 = sem("s_lo0")
        s_qkv = sem("s_qkv")
        s_qevac = sem("s_qevac")
        s_sc = sem("s_sc")
        s_soft = sem("s_soft")
        s_exp = sem("s_exp")
        s_pt = sem("s_pt")
        s_av = sem("s_av")
        s_ot = sem("s_ot")
        s_o = sem("s_o")
        s_ln = sem("s_ln")
        s_ve = sem("s_ve")
        s_rstd = sem("s_rstd")
        s_x1 = sem("s_x1")
        s_dup = sem("s_dup")
        s_acc = sem("s_acc")
        s_t1 = sem("s_t1")
        s_hi1 = sem("s_hi1")
        s_lo1 = sem("s_lo1")

        block = ctx.enter_context(nc.Block())

        @block.sync
        def _(sp):
            sp.dma_start(tokw[:, :, :], ins["tok_w"]).then_inc(s_tokw, 16)
            sp.dma_start(consts[:, :], ins["consts"]).then_inc(s_const, 16)

            def load_x(g, b):
                need(sp, s_e, g - 1)
                for t in range(GT):
                    sp.dma_start(xin[b][:, t, :, :], ins["patches"][bass.ds(g * GT + t, 1), :, :, :]
                                 .rearrange("o p c n -> (o p) c n")).then_inc(s_x[b], 16)

            load_x(0, 0)
            sp.dma_start(bo[:, :], ins["b_o"].to_broadcast([P, D])).then_inc(s_bo, 16)
            for j in range(3):
                need(sp, s_packl, j)
                sp.dma_start(wraw[:, :, :], ins["w_qkv"][j]).then_inc(s_wraw, 16)
                if j == 0:
                    load_x(1, 1)
                    sp.dma_start(wo[:, :, :], ins["w_o"]).then_inc(s_wo, 16)
                    sp.dma_start(graw[:, :, :], ins["gate_w"]).then_inc(s_graw, 16)
            with sp.Fori(1, NG // 2) as turn:
                for b in range(2):
                    load_x(turn * 2 + b, b)

        @block.gpsimd
        def _(pool):
            zeroed = [kT[b][r * H:r * H + H, :, 1 - r, :] for b in range(2) for r in range(2)]
            for k, part in enumerate(zeroed + [pT[t][:, :, :] for t in range(GT)]):
                need(pool, s_zero, k)
                pool.memset(part, 0.0).then_inc(s_zero, 1)
            pool.wait_ge(s_const, 16)

            def norm_group(g):
                held(pool, s_ln, 3 * GT * (g + 1))
                pool.tensor_scalar(vareps[:, :], meanvar[:, :, 1], EPS, None, ALU.add).then_inc(s_ve, 1)
                need(pool, s_ve, g + 1)
                need(pool, s_x1, g)
                pool.tensor_tensor(rstd[:, :], vareps[:, :], half, ALU.pow).then_inc(s_rstd, 1)
                held(pool, s_x1, g + 1)
                pool.tensor_copy(x1row[:, :, D:D + DB], x1row[:, :, P:D]).then_inc(s_dup, 1)
                pool.tensor_copy(acc[:, bass.ds(g * GT, GT), :], x1row[:, :, 0:D]).then_inc(s_acc, 1)

            norm_group(0)
            with pool.Fori(1, NG) as g:
                norm_group(g)

        @block.scalar
        def _(act):
            def copy_row(g):
                need(act, s_e, g + 1)
                need(act, s_t0, g)
                need(act, s_res, g)
                rows = p_row[:, 0:GT * D].rearrange("p (t d) -> p t d", t=GT)
                act.copy(h0row[:, :, 0:D], rows)
                act.copy(h0row[:, :, D:D + DB], rows[:, :, P:D]).then_inc(s_row, 1)

            def high0(g, b):
                need(act, s_t0, g + 1)
                act.copy(h0hi[b][:, :, :], p_row[:, :].rearrange("p (c n) -> p c n", c=2)).then_inc(s_hi0, 1)

            def high1(g):
                need(act, s_t1, g + 1)
                act.copy(XH[:, :, bass.ds(g * GTOK, GTOK)],
                         p_row[:, :].rearrange("p (c n) -> p c n", c=2)).then_inc(s_hi1, 1)

            def copy_qkv(g, b, item):
                need(act, s_qkv, ITEMS * g + item + 1)
                bank = p_qkv[item % 2]
                if item < IC // 2:
                    act.copy(qT[b][:, 2 * item:2 * item + 2, :], bank[:, :].rearrange("p (c n) -> p c n", c=2)) \
                       .then_inc(s_qevac, 1)
                elif item < IC:
                    c = 2 * (item - IC // 2)
                    for r in range(2):
                        act.copy(kT[b][r * H:r * H + H, c:c + 2, r, :],
                                 bank[r * H:r * H + H, :].rearrange("p (c n) -> p c n", c=2)) \
                           .then_inc(s_qevac, 1)
                else:
                    t, part = (item - IC) // 2, (item - IC) % 2
                    act.copy(v[b][:, t, part * F:part * F + F], bank[:, 0:F]).then_inc(s_qevac, 1)

            def exps(g, t):
                need(act, s_soft, 6 * (GT * g + t) + 3)
                need(act, s_pt, GT * g + t)
                act.activation(probs[:, :, :], scores[:, :, :], ACT.Exp).then_inc(s_exp, 1)

            def copy_ot(g, t):
                need(act, s_av, GT * g + t + 1)
                act.copy(oT[t][:, :, :], p_o[:, 0:INNER].rearrange("p (c n) -> p c n", c=IC)).then_inc(s_ot, 1)

            act.wait_ge(s_zero, 4 + GT)
            copy_row(0)
            high0(0, 0)
            for item in range(ITEMS):
                copy_qkv(0, 0, item)

            def body(g, b):
                nxt = not (isinstance(g, int) and g == NG - 1)
                if nxt:
                    copy_row(g + 1)
                exps(g, 0)
                if nxt:
                    high0(g + 1, 1 - b)
                    for item in range(IC // 2):
                        copy_qkv(g + 1, 1 - b, item)
                exps(g, 1)
                copy_ot(g, 0)
                if nxt:
                    for item in range(IC // 2, IC + 2):
                        copy_qkv(g + 1, 1 - b, item)
                copy_ot(g, 1)
                if not (isinstance(g, int) and g == 0):
                    high1(g - 1)
                if nxt:
                    for item in range(IC + 2, ITEMS):
                        copy_qkv(g + 1, 1 - b, item)

            pairs(act, NG, body)
            high1(NG - 1)

        @block.vector
        def _(dve):
            def residual(g):
                need(dve, s_row, g + 1)
                dve.tensor_tensor(acc[:, bass.ds(g * GT, GT), :], h0row[:, :, 0:D],
                                  bo[:, :].unsqueeze(1).to_broadcast([P, GT, D]), ALU.add).then_inc(s_res, 1)

            def low0(g, b):
                need(dve, s_hi0, g + 1)
                dve.tensor_tensor(h0lo[b][:, :, :], p_row[:, :].rearrange("p (c n) -> p c n", c=2),
                                  h0hi[b][:, :, :].bitcast(F32), ALU.subtract).then_inc(s_lo0, 1)

            def low1(g):
                need(dve, s_hi1, g + 1)
                cols = bass.ds(g * GTOK, GTOK)
                dve.tensor_tensor(XL[:, :, cols], p_row[:, :].rearrange("p (c n) -> p c n", c=2),
                                  XH[:, :, cols].bitcast(F32), ALU.subtract).then_inc(s_lo1, 1)

            def shift(g, t):
                n = GT * g + t
                need(dve, s_sc, n + 1)
                need(dve, s_exp, n)
                for q in range(4):
                    rows = slice(32 * q, 32 * q + 32)
                    last = dve.scalar_tensor_tensor(
                        out=scores[rows, :, :], in0=p_sc[rows, :, 32 * q:32 * q + 32], scalar=SCALE,
                        in1=mask[rows, :].unsqueeze(1).to_broadcast([32, HEADS, 32]), op0=ALU.mult, op1=ALU.add)
                last.then_inc(s_soft, 1)
                need(dve, s_soft, 6 * n + 1)
                dve.tensor_reduce(smax[:, :], scores[:, :, :], AX.X, ALU.max).then_inc(s_soft, 1)
                need(dve, s_soft, 6 * n + 2)
                dve.tensor_tensor(scores[:, :, :], scores[:, :, :],
                                  smax[:, :].unsqueeze(2).to_broadcast([P, HEADS, 32]), ALU.subtract) \
                   .then_inc(s_soft, 1)

            def normalise(g, t):
                n = GT * g + t
                need(dve, s_exp, n + 1)
                dve.tensor_reduce(ssum[:, :], probs[:, :, :], AX.X, ALU.add).then_inc(s_soft, 1)
                need(dve, s_soft, 6 * n + 4)
                dve.reciprocal(srec[:, :], ssum[:, :]).then_inc(s_soft, 1)
                need(dve, s_soft, 6 * n + 5)
                dve.tensor_tensor(probs[:, :, :], probs[:, :, :],
                                  srec[:, :].unsqueeze(2).to_broadcast([P, HEADS, 32]), ALU.mult) \
                   .then_inc(s_soft, 1)
                need(dve, s_soft, 6 * n + 6)
                need(dve, s_av, n - 1)
                for q in range(4):
                    rows = slice(32 * q, 32 * q + 32)
                    last = dve.transpose(pT[t][rows, :, 32 * q:32 * q + 32], probs[rows, :, :])
                last.then_inc(s_pt, 1)

            def add_residual(g, t):
                n = GT * g + t
                need(dve, s_o, n + 1)
                dve.tensor_tensor(z[t][:, :], p_o[:, 0:D],
                                  acc[:, bass.ds(g * GT + t, 1), :].rearrange("p o d -> p (o d)"), ALU.add) \
                   .then_inc(s_ln, 1)
                need(dve, s_ln, 3 * n + 1)
                dve.bn_stats(stats[:, t, :], z[t][:, :]).then_inc(s_ln, 1)
                held(dve, s_ln, 3 * n + 2)
                dve.bn_aggr(meanvar[:, t, :], stats[:, t, :]).then_inc(s_ln, 1)

            def norm_rows(g):
                need(dve, s_rstd, g + 1)
                need(dve, s_t1, g)
                need(dve, s_acc, g)
                for t in range(GT):
                    last = dve.tensor_scalar(x1row[:, t, 0:D], z[t][:, :], meanvar[:, t, 0:1], rstd[:, t:t + 1],
                                             ALU.subtract, ALU.mult)
                last.then_inc(s_x1, 1)

            dve.wait_ge(s_const, 16)
            dve.wait_ge(s_bo, 16)
            residual(0)
            for j in range(3):
                w = wqkv[:, :, j * INNER:(j + 1) * INNER]
                dve.wait_ge(s_wraw, 16 * (j + 1))
                pack_high(dve, w, wraw).then_inc(s_packh, 1)
                dve.wait_ge(s_packh, j + 1)
                pack_low(dve, w, wraw).then_inc(s_packl, 1)
                if j == 0:
                    low0(0, 0)
            dve.wait_ge(s_graw, 16)
            pack_high(dve, gate_pack, graw).then_inc(s_packh, 1)
            dve.wait_ge(s_packh, 4)
            pack_low(dve, gate_pack, graw).then_inc(s_packl, 1)
            dve.wait_ge(s_zero, 4 + GT)

            def body(g, b):
                nxt = not (isinstance(g, int) and g == NG - 1)
                if nxt:
                    residual(g + 1)
                shift(g, 0)
                if nxt:
                    low0(g + 1, 1 - b)
                normalise(g, 0)
                shift(g, 1)
                normalise(g, 1)
                add_residual(g, 0)
                if not (isinstance(g, int) and g == 0):
                    low1(g - 1)
                add_residual(g, 1)
                norm_rows(g)

            pairs(dve, NG, body)
            low1(NG - 1)

        @block.tensor
        def _(pe):
            def embed(g, b):
                need(pe, s_x[b], 16 * GT * ((g - b) // 2 + 1))
                need(pe, s_hi0, g)
                need(pe, s_lo0, g)
                if not isinstance(g, int) or g >= 3:
                    pe.wait_ge(s_hi1, g - 2)
                    pe.wait_ge(s_lo1, g - 2)
                for t in range(GT):
                    for c in range(KC):
                        mm = pe.matmul(p_row[:, t * D:t * D + D], xin[b][:, t, c, :], tokw[:, c, :],
                                       start=(c == 0), stop=(c == KC - 1))
                mm.then_inc(s_e, 1)

            def turn_rows(rows):
                for c in range(2):
                    for t in range(GT):
                        mm = pe.transpose(p_row[:, (c * GT + t) * P:(c * GT + t + 1) * P],
                                          rows[:, t, c * P:(c + 1) * P], ident)
                return mm

            def transpose0(g):
                need(pe, s_row, g + 1)
                turn_rows(h0row).then_inc(s_t0, 1)

            def transpose1(g):
                need(pe, s_dup, g + 1)
                after = min(g + 3, NG) if isinstance(g, int) else g + 3
                need(pe, s_hi0, after)
                need(pe, s_lo0, after)
                need(pe, s_hi1, g)
                need(pe, s_lo1, g)
                turn_rows(x1row).then_inc(s_t1, 1)

            def qkv(g, b, item):
                if item == 0:
                    need(pe, s_hi0, g + 1)
                    need(pe, s_lo0, g + 1)
                done = [1, 2, 3, 5, 7, 9, 10, 11, 12, 13][(item - 2) % ITEMS]
                need(pe, s_qevac, EVACS * (g if item >= 2 else g - 1) + done)
                bank = p_qkv[item % 2]
                xh, xl = h0hi[b], h0lo[b]
                if item < IC:
                    for j in range(2):
                        c = 2 * item + j
                        terms = stack_terms(wqkv[:, :, c * P:(c + 1) * P], xh, xl)
                        for k, (w, x) in enumerate(terms):
                            mm = pe.matmul(bank[:, j * GTOK:(j + 1) * GTOK], w, x,
                                           start=(k == 0), stop=(k == len(terms) - 1))
                else:
                    t, part = (item - IC) // 2, (item - IC) % 2
                    col = 2 * INNER + part * F
                    cols = slice(t * P, t * P + P)
                    terms = stack_terms(wqkv[:, :, col:col + F], xh[:, :, cols], xl[:, :, cols])
                    for k, (w, x) in enumerate(terms):
                        mm = pe.matmul(bank[:, 0:F], x, w, start=(k == 0), stop=(k == len(terms) - 1))
                mm.then_inc(s_qkv, 1)

            def score(g, b, t):
                need(pe, s_qevac, EVACS * g + 3 * (IC // 2))
                need(pe, s_soft, 6 * (GT * g + t - 1) + 1)
                cols = slice(t * P, t * P + P)
                for c in range(IC):
                    mm = pe.matmul(p_sc[:, 2 * c:2 * c + 2, :], qT[b][:, c, cols], kT[b][:, c, :, cols],
                                   start=True, stop=True)
                mm.then_inc(s_sc, 1)

            def attend(g, b, t):
                n = GT * g + t
                need(pe, s_qevac, EVACS * (g + 1))
                need(pe, s_pt, n + 1)
                need(pe, s_ln, 3 * (n - 1) + 1)
                for h in range(HEADS):
                    r = (h % 2) * H
                    mm = pe.matmul(p_o[r:r + H, (h // 2) * P:(h // 2 + 1) * P], v[b][:, t, h * DH:(h + 1) * DH],
                                   pT[t][:, h, :], start=True, stop=True)
                mm.then_inc(s_av, 1)

            def project(g, t):
                need(pe, s_ot, GT * g + t + 1)
                for c in range(IC):
                    mm = pe.matmul(p_o[:, 0:D], oT[t][:, c, :], wo[:, c, :], start=(c == 0), stop=(c == IC - 1))
                mm.then_inc(s_o, 1)

            pe.wait_ge(s_tokw, 16)
            pe.wait_ge(s_const, 16)
            embed(0, 0)
            transpose0(0)
            for item in range(ITEMS):
                pe.wait_ge(s_packl, min(3, 1 + item // (IC // 2)))
                qkv(0, 0, item)
            pe.wait_ge(s_zero, 4 + GT)
            pe.wait_ge(s_wo, 16)

            def body(g, b):
                nxt = not (isinstance(g, int) and g == NG - 1)
                if nxt:
                    embed(g + 1, 1 - b)
                score(g, b, 0)
                if nxt:
                    transpose0(g + 1)
                score(g, b, 1)
                if nxt:
                    for item in range(IC // 2):
                        qkv(g + 1, 1 - b, item)
                attend(g, b, 0)
                if nxt:
                    for item in range(IC // 2, IC):
                        qkv(g + 1, 1 - b, item)
                project(g, 0)
                if nxt:
                    for item in range(IC, IC + 2):
                        qkv(g + 1, 1 - b, item)
                attend(g, b, 1)
                if not (isinstance(g, int) and g == 0):
                    transpose1(g - 1)
                project(g, 1)
                if nxt:
                    for item in range(IC + 2, ITEMS):
                        qkv(g + 1, 1 - b, item)

            pairs(pe, NG, body)
            transpose1(NG - 1)


def experts(nc, ins, consts, gate_pack, XH, XL, acc, out):
    with ExitStack() as ctx:
        def sb(name, shape, dt=F32):
            return ctx.enter_context(nc.sbuf_tensor(name, shape, dt))

        def ps(name, shape):
            return ctx.enter_context(nc.psum_tensor(name, shape, F32))

        def sem(name):
            return ctx.enter_context(nc.semaphore(name))

        w2 = sb("w2", [P, E, FC, D])
        fb1 = [sb(f"fb1{b}", [P, FC]) for b in range(2)]
        lnw = sb("lnw", [P, E, FC])
        lnb = sb("lnb", [P, E, FC])
        gateb = sb("gateb", [P, E])
        fb2 = sb("fb2", [P, D])
        w1raw = [sb(f"w1raw{b}", [P, 2, F]) for b in range(2)]
        w1p = [sb(f"w1p{b}", [P, 4, F], F32R) for b in range(2)]
        w2s = sb("w2s", [P, FC, D])
        w2c = sb("w2c", [P, FC, D])
        c_hi = [sb(f"c_hi{b}", [P, FC, CW], F32R) for b in range(2)]
        c_lo = [sb(f"c_lo{b}", [P, FC, CW], F32R) for b in range(2)]
        g = [sb(f"g{b}", [P, FC, STOK]) for b in range(2)]
        g_hi = [sb(f"g_hi{b}", [P, FC, STOK], F32R) for b in range(2)]
        g_lo = [sb(f"g_lo{b}", [P, FC, STOK], F32R) for b in range(2)]
        sq = sb("sq", [P, FC, STOK])
        sq01 = sb("sq01", [P, STOK])
        sqsum = [sb(f"sqsum{b}", [P, STOK]) for b in range(2)]
        sums = [sb(f"sums{b}", [P, ST, 2]) for b in range(2)]
        sumg2 = sb("sumg2", [P, ST])
        sqn = sb("sqn", [P, ST])
        varn = sb("varn", [P, ST])
        vare = sb("vare", [P, ST])
        rn = sb("rn", [P, ST])
        scale = [sb(f"scale{b}", [P, ST]) for b in range(2)]
        logit = sb("logit", [P, NT, E])
        lmax = sb("lmax", [P, NT])
        lsum = sb("lsum", [P, NT])
        lrec = sb("lrec", [P, NT])
        prob = sb("prob", [P, NT, E + 8])
        top8 = sb("top8", [P, NT, 8])
        marked = sb("marked", [P, NT, E + 8])
        comb = sb("comb", [P, NT, E])
        combn = sb("combn", [P, E, NT])
        combT = sb("combT", [P, 2, P])
        lnbx = sb("lnbx", [P, FC, E, P])
        crep = sb("crep", [P, D])
        crows = sb("crows", [P, 8, D])
        st2 = sb("st2", [P, NT, 6])
        mv2 = sb("mv2", [P, NT, 2])
        ve2 = sb("ve2", [P, NT])
        rs2 = sb("rs2", [P, NT])
        res = w2[:, :, 0, :]

        p_h = [ps(f"p_h{f}", [P, STOK]) for f in range(FC)]
        p_w = ps("p_w", [P, 512])
        p_y = [ps(f"p_y{b}", [P, ST, YW]) for b in range(2)]

        ident = consts[:, C_ID:C_ID + P]
        ones = consts[:, C_ONES:C_ONES + P]
        rowmask = consts[:, C_ROW:C_ROW + 8]
        half = consts[:, C_HALF:C_HALF + NT]

        s_w1 = [sem(f"s_w1raw{b}") for b in range(2)]
        s_b1 = [sem(f"s_b1{b}") for b in range(2)]
        s_small = sem("s_small")
        s_w2 = sem("s_w2")
        s_ph = sem("s_ph")
        s_w1p = sem("s_w1p")
        s_w2s = sem("s_w2s")
        s_mean = sem("s_mean")
        s_cen = sem("s_cen")
        s_chi = sem("s_chi")
        s_cp = sem("s_cp")
        s_pad = sem("s_pad")
        s_router = sem("s_router")
        s_r = sem("s_r")
        s_rexp = sem("s_rexp")
        s_lnbx = sem("s_lnbx")
        s_const2 = sem("s_const2")
        s_crow = sem("s_crow")
        s_combt = sem("s_combt")
        s_combs = sem("s_combs")
        s_init = sem("s_init")
        s_initd = sem("s_initd")
        s_g1 = sem("s_g1")
        s_gelu = sem("s_gelu")
        s_sq = sem("s_sq")
        s_sq01 = sem("s_sq01")
        s_sqs = sem("s_sqs")
        s_hi = sem("s_hi")
        s_lo = sem("s_lo")
        s_y = sem("s_y")
        s_sums = sem("s_sums")
        s_v = sem("s_v")
        s_scale = sem("s_scale")
        s_ev = sem("s_ev")
        s_f = sem("s_f")
        s_fa = sem("s_fa")
        s_fp = sem("s_fp")
        s_res = sem("s_res2")
        s_out = sem("s_out")

        block = ctx.enter_context(nc.Block())

        @block.sync
        def _(sp):
            def load_w1(e, b):
                need(sp, s_gelu, FC * NQ * (e - 1))
                sp.dma_start(fb1[b][:, :], ins["fc1_b"][bass.ds(e, 1), :, :].rearrange("o p c -> (o p) c")) \
                   .then_inc(s_b1[b], 16)
                need(sp, s_w1p, e - 1)
                sp.dma_start(w1raw[b][:, :, :], ins["fc1_w"][bass.ds(e, 1), :, :, :]
                             .rearrange("o p c n -> (o p) c n")).then_inc(s_w1[b], 16)

            load_w1(0, 0)
            sp.dma_start(gateb[:, :], ins["gate_b"].to_broadcast([P, E])).then_inc(s_small, 16)
            sp.dma_start(lnw[:, :, :], ins["ln_w"]).then_inc(s_small, 16)
            sp.dma_start(lnb[:, :, :], ins["ln_b"]).then_inc(s_small, 16)
            sp.dma_start(fb2[:, :], ins["fc2_b"]).then_inc(s_small, 16)
            sp.dma_start(w2[:, :, :, :], ins["fc2_w"]).then_inc(s_w2, 16)
            load_w1(1, 1)
            with sp.Fori(1, E // 2) as turn:
                for b in range(2):
                    load_w1(turn * 2 + b, b)
            for t in range(NT):
                sp.wait_ge(s_res, t + 1)
                sp.dma_start(out[t * P:(t + 1) * P, :], res[:, t, :]).then_inc(s_out, 16)
            sp.wait_ge(s_out, 16 * NT)

        @block.gpsimd
        def _(pool):
            for b in range(2):
                pool.memset(c_hi[b][:, :, D:D + 1].bitcast(F32), 1.0)
                pool.memset(c_hi[b][:, :, D + 1:CW].bitcast(F32), 0.0)
                last = pool.memset(c_lo[b][:, :, D:CW].bitcast(F32), 0.0)
            last.then_inc(s_pad, 1)
            pool.wait_ge(s_small, 64)
            pool.wait_ge(s_w2, 16)

            def scale_w2(e):
                need(pool, s_cen, e)
                pool.tensor_tensor(w2s[:, :, :], w2[:, bass.ds(e, 1), :, :].rearrange("p o c d -> p (o c) d"),
                                   lnw[:, bass.ds(e, 1), :].rearrange("p o c -> p (o c)")
                                   .unsqueeze(2).to_broadcast([P, FC, D]), ALU.mult).then_inc(s_w2s, 1)

            def sum_squares(i, b):
                need(pool, s_sq, i + 1)
                need(pool, s_sqs, i)
                pool.tensor_tensor(sq01[:, :], sq[:, 0, :], sq[:, 1, :], ALU.add).then_inc(s_sq01, 1)
                need(pool, s_sq01, i + 1)
                need(pool, s_y, i - 1)
                pool.tensor_tensor(sqsum[b][:, :], sq01[:, :], sq[:, 2, :], ALU.add).then_inc(s_sqs, 1)

            def factors(i, b, e, q):
                held(pool, s_sums, i + 1)
                pool.tensor_tensor(sumg2[:, :], sums[b][:, :, 0], sums[b][:, :, 0], ALU.mult)
                pool.tensor_scalar(sqn[:, :], sums[b][:, :, 1], float(F), None, ALU.mult).then_inc(s_v, 1)
                need(pool, s_v, 4 * i + 1)
                pool.tensor_tensor(varn[:, :], sqn[:, :], sumg2[:, :], ALU.subtract).then_inc(s_v, 1)
                held(pool, s_v, 4 * i + 2)
                pool.tensor_scalar(vare[:, :], varn[:, :], 0.0, EPS * F * F, ALU.max, ALU.add).then_inc(s_v, 1)
                need(pool, s_v, 4 * i + 3)
                pool.tensor_tensor(rn[:, :], vare[:, :], half[:, 0:ST], ALU.pow).then_inc(s_v, 1)
                need(pool, s_v, 4 * i + 4)
                need(pool, s_ev, i - 1)
                pool.tensor_tensor(scale[b][:, :], rn[:, :],
                                   combn[:, bass.ds(e, 1), q * ST:(q + 1) * ST].rearrange("p o t -> p (o t)"),
                                   ALU.mult).then_inc(s_scale, 1)

            scale_w2(0)
            sum_squares(0, 0)
            pool.wait_ge(s_r, R_COMBN)

            def body(e, b):
                last = isinstance(e, int) and e == E - 1
                for q in range(NQ):
                    i = e * NQ + q
                    if not (last and q == NQ - 1):
                        sum_squares(i + 1, (q + 1) % 2)
                    factors(i, q % 2, e, q)
                    if q == 0 and not last:
                        scale_w2(e + 1)

            pairs(pool, E, body)
            pool.wait_ge(s_fa, NT)
            pool.tensor_scalar(ve2[:, :], mv2[:, :, 1], EPS, None, ALU.add).then_inc(s_fp, 1)
            pool.wait_ge(s_fp, 1)
            pool.tensor_tensor(rs2[:, :], ve2[:, :], half, ALU.pow).then_inc(s_fp, 1)

        @block.scalar
        def _(act):
            act.wait_ge(s_r, 3)
            act.activation(prob[:, :, 0:E], logit[:, :, :], ACT.Exp).then_inc(s_rexp, 1)

            def gelus(i, b, e_b):
                for f in range(FC):
                    need(act, s_g1, FC * i + f + 1)
                    need(act, s_lo, FC * (i - 2) + f + 1)
                    if f == 0:
                        need(act, s_sq, i - 1)
                    act.activation(g[b][:, f, :], p_h[f][:, :], ACT.Gelu,
                                   bias=fb1[e_b][:, f:f + 1]) \
                       .then_inc(s_gelu, 1)
                need(act, s_gelu, FC * (i + 1))
                need(act, s_sqs, i)
                act.activation(sq[:, :, :], g[b][:, :, :], ACT.Square).then_inc(s_sq, 1)

            def body(e, b):
                need(act, s_b1[b], 16 * ((e - b) // 2 + 1))
                for q in range(NQ):
                    gelus(e * NQ + q, q % 2, b)

            pairs(act, E, body)

        @block.vector
        def _(dve):
            def pack_w1(e, b):
                need(dve, s_w1[b], 16 * ((e - b) // 2 + 1))
                need(dve, s_g1, FC * NQ * (e - 1))
                pack_high(dve, w1p[b], w1raw[b]).then_inc(s_ph, 1)
                need(dve, s_ph, e + 1)
                pack_low(dve, w1p[b], w1raw[b]).then_inc(s_w1p, 1)

            def pack_w2(e, b):
                need(dve, s_mean, e + 1)
                dve.scalar_tensor_tensor(out=w2c[:, :, :], in0=p_w[:, 0:D].unsqueeze(1).to_broadcast([P, FC, D]),
                                         scalar=-1.0 / F, in1=w2s[:, :, :], op0=ALU.mult, op1=ALU.add) \
                   .then_inc(s_cen, 1)
                need(dve, s_cen, e + 1)
                need(dve, s_y, NQ * (e - 1))
                dve.tensor_copy(c_hi[b][:, :, 0:D], w2c[:, :, :]).then_inc(s_chi, 1)
                need(dve, s_chi, e + 1)
                dve.tensor_tensor(c_lo[b][:, :, 0:D], w2c[:, :, :], c_hi[b][:, :, 0:D].bitcast(F32),
                                  ALU.subtract).then_inc(s_cp, 1)

            def split(i, b):
                for f in range(FC):
                    n = FC * i + f + 1
                    need(dve, s_gelu, n)
                    if f == 0:
                        need(dve, s_y, i - 1)
                    dve.tensor_copy(g_hi[b][:, f, :], g[b][:, f, :]).then_inc(s_hi, 1)
                    need(dve, s_hi, n)
                    dve.tensor_tensor(g_lo[b][:, f, :], g[b][:, f, :], g_hi[b][:, f, :].bitcast(F32),
                                      ALU.subtract).then_inc(s_lo, 1)

            def copy_sums(i, b):
                need(dve, s_y, i + 1)
                need(dve, s_v, 4 * (i - 2) + 1)
                dve.tensor_copy(sums[b][:, :, :], p_y[b][:, :, SUMG:SUMSQ + 1:2]).then_inc(s_sums, 1)

            def add_out(i, b, q):
                need(dve, s_scale, i + 1)
                need(dve, s_ev, i - NQ + 1)
                for t in range(ST):
                    tile = acc[:, q * ST + t, :]
                    last = dve.scalar_tensor_tensor(out=tile, in0=p_y[b][:, t, 0:D], scalar=scale[b][:, t:t + 1],
                                                    in1=tile, op0=ALU.mult, op1=ALU.add)
                last.then_inc(s_ev, 1)

            step = [0]

            def r(ins):
                step[0] += 1
                ins.then_inc(s_r, 1)
                dve.wait_ge(s_r, step[0])

            dve.wait_ge(s_small, 64)
            dve.wait_ge(s_router, 1)
            dve.tensor_tensor(logit[:, :, :], p_w[:, 0:NT * E].rearrange("p (t e) -> p t e", t=NT),
                              gateb[:, :].unsqueeze(1).to_broadcast([P, NT, E]), ALU.add).then_inc(s_r, 1)
            step[0] += 1
            dve.memset(prob[:, :, E:E + 8], -1.0)
            dve.wait_ge(s_r, 1)
            r(dve.memset(logit[:, :, 0:SHARED], NEG_INF))
            dve.tensor_reduce(lmax[:, :], logit[:, :, :], AX.X, ALU.max).then_inc(s_f, 1)
            dve.wait_ge(s_f, 1)
            r(dve.tensor_tensor(logit[:, :, :], logit[:, :, :], lmax[:, :].unsqueeze(2).to_broadcast([P, NT, E]),
                                ALU.subtract))
            pack_w1(0, 0)
            for e in range(E):
                last = dve.tensor_tensor(lnbx[:, :, e, :], lnb[:, e, :].unsqueeze(2).to_broadcast([P, FC, P]),
                                         eye_row(consts, e), ALU.mult)
            last.then_inc(s_lnbx, 1)
            dve.wait_ge(s_rexp, 1)
            r(dve.tensor_reduce(lsum[:, :], prob[:, :, 0:E], AX.X, ALU.add))
            r(dve.reciprocal(lrec[:, :], lsum[:, :]))
            r(dve.tensor_tensor(prob[:, :, 0:E], prob[:, :, 0:E], lrec[:, :].unsqueeze(2).to_broadcast([P, NT, E]),
                                ALU.mult))
            for t in range(NT):
                last = dve.max(top8[:, t, :], prob[:, t, :])
            r(last)
            r(dve.memset(top8[:, :, ROUTE:8], -1.0))
            for t in range(NT):
                last = dve.match_replace(marked[:, t, :], top8[:, t, :], prob[:, t, :], -2.0)
            r(last)
            r(dve.scalar_tensor_tensor(out=comb[:, :, :], in0=marked[:, :, 0:E], scalar=-2.0, in1=prob[:, :, 0:E],
                                       op0=ALU.is_equal, op1=ALU.mult))
            r(dve.tensor_scalar(comb[:, :, 0:SHARED], comb[:, :, 0:SHARED], 1.0, None, ALU.add))
            r(dve.tensor_scalar(combn[:, :, :].rearrange("p e t -> p t e"), comb[:, :, :], float(F), None, ALU.mult))
            assert step[0] == R_COMBN
            split(0, 0)
            dve.wait_ge(s_const2, 1)
            dve.tensor_tensor(crep[:, :], p_w[:, 256:256 + D], fb2[:, :], ALU.add).then_inc(s_crow, 1)
            dve.wait_ge(s_pad, 1)
            pack_w2(0, 0)
            dve.wait_ge(s_crow, 1)
            dve.tensor_tensor(crows[:, :, :], crep[:, :].unsqueeze(1).to_broadcast([P, 8, D]),
                              rowmask.unsqueeze(2).to_broadcast([P, 8, D]), ALU.mult).then_inc(s_crow, 1)
            dve.wait_ge(s_combt, 1)
            dve.tensor_copy(combT[:, :, :], p_y[1][:, 0, :].rearrange("p (c n) -> p c n", c=2)).then_inc(s_combs, 1)
            for j in range(NT // 4):
                dve.wait_ge(s_init, j + 1)
                dve.tensor_tensor(acc[:, 4 * j:4 * j + 4, :], p_y[j % 2][:, :, 0:D], acc[:, 4 * j:4 * j + 4, :],
                                  ALU.add).then_inc(s_initd, 1)
            dve.wait_ge(s_initd, NT // 4)

            def body(e, b):
                last = isinstance(e, int) and e == E - 1
                first = isinstance(e, int) and e == 0
                for q in range(NQ):
                    i = e * NQ + q
                    if q == 0 and not last:
                        pack_w1(e + 1, 1 - b)
                    if not (last and q == NQ - 1):
                        split(i + 1, (q + 1) % 2)
                    copy_sums(i, q % 2)
                    if not (first and q == 0):
                        add_out(i - 1, (q + 1) % 2, (q - 1) % NQ)
                    if q == 2 and not last:
                        pack_w2(e + 1, 1 - b)

            pairs(dve, E, body)
            add_out(STEPS - 1, (NQ - 1) % 2, NQ - 1)
            dve.wait_ge(s_ev, STEPS)
            for t in range(NT):
                dve.bn_stats(st2[:, t, :], acc[:, t, :]).then_inc(s_f, 1)
            for t in range(NT):
                dve.wait_ge(s_f, 2 + t)
                dve.bn_aggr(mv2[:, t, :], st2[:, t, :]).then_inc(s_fa, 1)
            dve.wait_ge(s_fp, 2)
            for t in range(NT):
                dve.tensor_scalar(res[:, t, :], acc[:, t, :], mv2[:, t, 0:1], rs2[:, t:t + 1],
                                  ALU.subtract, ALU.mult).then_inc(s_res, 1)

        @block.tensor
        def _(pe):
            def hidden(i, b, q):
                cols = slice(q * STOK, (q + 1) * STOK)
                for f in range(FC):
                    need(pe, s_gelu, FC * (i - 1) + f + 1)
                    terms = stack_terms(w1p[b][:, :, f * P:(f + 1) * P], XH[:, :, cols], XL[:, :, cols])
                    for k, (w, x) in enumerate(terms):
                        mm = pe.matmul(p_h[f][:, :], w, x, start=(k == 0), stop=(k == len(terms) - 1))
                    mm.then_inc(s_g1, 1)

            def outputs(i, b, sb_):
                need(pe, s_lo, FC * (i + 1))
                need(pe, s_sqs, i + 1)
                need(pe, s_ev, i - 1)
                for t in range(ST):
                    cols = slice(t * P, t * P + P)
                    for f in range(FC):
                        for k, (gx, wx) in enumerate(((g_hi, c_hi), (g_hi, c_lo), (g_lo, c_hi))):
                            pe.matmul(p_y[sb_][:, t, 0:CW], gx[sb_][:, f, cols], wx[b][:, f, :],
                                      start=(t % 2 == 0 and f == 0 and k == 0), stop=(f == FC - 1 and k == 2),
                                      skip_group_check=True)
                    mm = pe.matmul(p_y[sb_][:, t, SUMSQ:SUMSQ + 1], sqsum[sb_][:, cols], ones[:, 0:1],
                                   start=False, stop=True, skip_group_check=True)
                mm.then_inc(s_y, 1)

            def column_sums(e):
                need(pe, s_w2s, e + 1)
                need(pe, s_cen, e)
                for f in range(FC):
                    mm = pe.matmul(p_w[:, 0:D], ones, w2s[:, f, :], start=(f == 0), stop=(f == FC - 1))
                mm.then_inc(s_mean, 1)

            for t in range(NT):
                cols = slice(t * P, t * P + P)
                terms = stack_terms(gate_pack, XH[:, :, cols], XL[:, :, cols])
                for k, (w, x) in enumerate(terms):
                    mm = pe.matmul(p_w[:, t * E:(t + 1) * E], x, w, start=(k == 0), stop=(k == len(terms) - 1))
            mm.then_inc(s_router, 1)
            pe.wait_ge(s_w1p, 1)
            hidden(0, 0, 0)
            pe.wait_ge(s_w2, 16)
            pe.wait_ge(s_lnbx, 1)
            pe.wait_ge(s_r, 1)
            for e in range(E):
                for f in range(FC):
                    mm = pe.matmul(p_w[:, 256:256 + D], lnbx[:, f, e, :], w2[:, e, f, :],
                                   start=(e == 0 and f == 0), stop=(e == E - 1 and f == FC - 1))
            mm.then_inc(s_const2, 1)
            pe.wait_ge(s_crow, 1)
            column_sums(0)
            pe.wait_ge(s_r, R_COMBN)
            for j in range(2):
                mm = pe.transpose(p_y[1][:, 0, j * P:(j + 1) * P],
                                  comb[:, 8 * j:8 * j + 8, :].rearrange("p t e -> p (t e)"), ident)
            mm.then_inc(s_combt, 1)
            pe.wait_ge(s_crow, 2)
            pe.wait_ge(s_combs, 1)
            for t in range(NT):
                if t % 4 == 0:
                    need(pe, s_initd, t // 4 - 1)
                mm = pe.matmul(p_y[(t // 4) % 2][:, t % 4, 0:D], combT[:, t // 8, :], crows[:, t % 8, :],
                               start=True, stop=True)
                if t % 4 == 3:
                    mm.then_inc(s_init, 1)
            pe.wait_ge(s_initd, NT // 4)

            def body(e, b):
                last = isinstance(e, int) and e == E - 1
                for q in range(NQ):
                    i = e * NQ + q
                    if q < NQ - 1:
                        hidden(i + 1, b, q + 1)
                    elif not last:
                        need(pe, s_w1p, e + 2)
                        hidden(i + 1, 1 - b, 0)
                    if q == 0:
                        need(pe, s_cp, e + 1)
                    outputs(i, b, q % 2)
                    if q == 1 and not last:
                        column_sums(e + 1)

            pairs(pe, E, body)


R_COMBN = 12


def eye_row(consts, e):
    return consts[:, C_EYE + E - e:C_EYE + E - e + P].unsqueeze(1).to_broadcast([P, FC, P])


def vit_layer(nc, ins, out):
    with ExitStack() as ctx:
        def sb(name, shape, dt=F32):
            return ctx.enter_context(nc.sbuf_tensor(name, shape, dt))

        consts = sb("consts", [P, C_END])
        gate_pack = sb("gate_pack", [P, 4, E], F32R)
        XH = sb("XH", [P, 2, TOK], F32R)
        XL = sb("XL", [P, 2, TOK], F32R)
        acc = sb("acc", [P, NT, D])
        attention(nc, ins, consts, gate_pack, XH, XL, acc)
        experts(nc, ins, consts, gate_pack, XH, XL, acc, out)


def kernel(**inputs):
    import numpy as np
    import concourse.bacc as bacc
    from concourse.bass_utils import run_bass_kernel_spmd

    a = {k: np.asarray(x) for k, x in inputs.items()}

    def doubled(w):
        return np.stack([w[:P], np.concatenate([w[P:], w[P:]])], axis=1)

    def by_chunk(w, c):
        return w.reshape(c, P, -1).transpose(1, 0, 2)

    x = a["x"].reshape(IMAGES, CHANNELS, SIDE // PATCH, PATCH, SIDE // PATCH, PATCH)
    x = x.transpose(3, 5, 1, 0, 2, 4).reshape(KC, P, NT, P).transpose(2, 1, 0, 3)
    consts = np.zeros((P, C_END), np.float32)
    consts[:, C_ID:C_ID + P] = np.eye(P)
    rows = np.arange(P)
    other = (rows[:, None] % 32) // SEQ != np.arange(32)[None, :] // SEQ
    consts[:, C_MASK:C_MASK + 32][other] = MASKED
    consts[:, C_ONES:C_ONES + P] = 1.0
    consts[:, C_ROW:C_ROW + 8] = rows[:, None] // E == np.arange(8)[None, :]
    consts[:, C_HALF:C_END] = -0.5
    consts[:, C_EYE:C_EYE + P + E:E] = 1.0
    arrays = {
        "consts": consts,
        "patches": x,
        "tok_w": by_chunk(a["L0_tok_W"], KC),
        "w_qkv": np.stack([doubled(a[f"L0_attn_w_{n}"]) for n in "qkv"]),
        "w_o": by_chunk(a["L0_attn_w_o"], IC),
        "b_o": a["L0_attn_b_o"].reshape(1, D),
        "gate_w": doubled(a["L0_ffn_gate_w"]),
        "gate_b": a["L0_ffn_gate_b"].reshape(1, E),
        "fc1_w": np.stack([doubled(w) for w in a["L0_ffn_fc1_w"]]),
        "fc1_b": a["L0_ffn_fc1_b"].reshape(E, FC, P).transpose(0, 2, 1),
        "ln_w": a["L0_ffn_ln_w"].reshape(E, FC, P).transpose(2, 0, 1),
        "ln_b": a["L0_ffn_ln_b"].reshape(E, FC, P).transpose(2, 0, 1),
        "fc2_w": a["L0_ffn_fc2_w"].reshape(E, FC, P, D).transpose(2, 0, 1, 3),
        "fc2_b": np.concatenate([a["L0_ffn_fc2_b"]] * 8),
    }
    arrays = {k: np.ascontiguousarray(w) for k, w in arrays.items()}
    nc = bacc.Bacc("TRN2", target_bir_lowering=False, num_devices=1)
    ins = {k: nc.dram_tensor(f"in_{k}", w.shape, F32, kind="ExternalInput").ap() for k, w in arrays.items()}
    out = nc.dram_tensor("out_0", (IMAGES, SEQ, D), F32, kind="ExternalOutput").ap()
    vit_layer(nc, ins, out.rearrange("b n d -> (b n) d"))
    r = run_bass_kernel_spmd(nc, [{f"in_{k}": w for k, w in arrays.items()}], core_ids=[0])
    return r.results[0]["out_0"]
```

```python
from contextlib import ExitStack

import concourse.bass as bass
from concourse import mybir

F32 = mybir.dt.float32
F32R = mybir.dt.float32r
ALU = mybir.AluOpType
ACT = mybir.ActivationFunctionType
AX = mybir.AxisListType

P = 128
H = 64
PATCH = 16
IMAGES, CHANNELS, SIDE = 128, 3, 64
SEQ = (SIDE // PATCH) ** 2
TOK = IMAGES * SEQ
NT = TOK // P
KC = CHANNELS * PATCH * PATCH // P
D = 192
DB = D - P
HEADS, DH = 12, 64
INNER = HEADS * DH
IC = INNER // P
SCALE = 1.0 / 8.0
MASKED = -1e30
E = 16
F = 384
FC = F // P
SHARED, ROUTE = 1, 3
NEG_INF = -1e9
EPS = 1e-5

GT = 2
GTOK = GT * P
NG = NT // GT
ST = 4
STOK = ST * P
NQ = NT // ST
STEPS = E * NQ
YW = 256
CW = D + 2
SUMG, SUMSQ = D, D + 2
ITEMS = 2 * FC + 2 * GT
NQK = 2 * IC // 2
EVACS = IC // 2 + 2 * (IC // 2) + 2 * GT

C_ID, C_MASK, C_ONES, C_EYE, C_ROW, C_HALF, C_QUAD, C_FOLD, C_END = 0, 128, 160, 288, 432, 440, 456, 460, 588


def need(eng, sem, count):
    if not (isinstance(count, int) and count <= 0):
        eng.wait_ge(sem, count)


def held(eng, sem, count):
    need(eng, sem, count)
    eng.nop(nofuse=True)


def pairs(eng, n, body):
    for k in (0, 1):
        body(k, k)
    with eng.Fori(1, n // 2 - 1) as turn:
        for k in (0, 1):
            body(turn * 2 + k, k)
    for k in (n - 2, n - 1):
        body(k, k % 2)


def stack_terms(w, xh, xl):
    return [(w[:, 0, :], xh[:, 0, :]), (w[:, 0, :], xl[:, 0, :]), (w[:, 1, :], xh[:, 0, :]),
            (w[:, 2, :], xh[:, 1, :]), (w[:, 3, :], xl[:, 1, :])]


def pack_high(dve, w, raw):
    dve.tensor_copy(w[:, 0, :], raw[:, 0, :])
    dve.tensor_copy(w[0:H, 2, :], raw[0:H, 1, :])
    return dve.tensor_copy(w[H:P, 3, :], raw[H:P, 1, :])


def pack_low(dve, w, raw):
    dve.tensor_tensor(w[:, 1, :], raw[:, 0, :], w[:, 0, :].bitcast(F32), ALU.subtract)
    dve.tensor_tensor(w[H:P, 2, :], raw[H:P, 1, :], w[H:P, 3, :].bitcast(F32), ALU.subtract)
    return dve.tensor_tensor(w[0:H, 3, :], raw[0:H, 1, :], w[0:H, 2, :].bitcast(F32), ALU.subtract)


def attention(nc, ins, consts, gate_pack, XH, XL, acc, logit, crep, lnb, lnw, fb1, wbuf, w1p0, w2raw):
    with ExitStack() as ctx:
        def sb(name, shape, dt=F32):
            return ctx.enter_context(nc.sbuf_tensor(name, shape, dt))

        def ps(name, shape):
            return ctx.enter_context(nc.psum_tensor(name, shape, F32))

        def sem(name):
            return ctx.enter_context(nc.semaphore(name))

        xin = [sb(f"xin{b}", [P, GT, KC, P]) for b in range(2)]
        tokw = sb("tokw", [P, KC, D])
        wraw = [wbuf[:, :].rearrange("p (c n) -> p c n", c=2)] + \
            [acc[:, j * NT // 2:(j + 1) * NT // 2, :].rearrange("p t d -> p (t d)").rearrange("p (c n) -> p c n", c=2)
             for j in range(2)]
        lnbx = sb("lnbx", [P, FC, P])
        logitT = sb("logitT", [E, GTOK])
        gateb = sb("gateb", [P, E])
        graw = sb("graw", [P, 2, E])
        wqkv = sb("wqkv", [P, 4, 3 * INNER], F32R)
        wo = sb("wo", [P, IC, D])
        bo = sb("bo", [P, D])
        h0row = sb("h0row", [P, GT, D + DB])
        h0hi = [sb(f"h0hi{b}", [P, 2, GTOK], F32R) for b in range(2)]
        h0lo = [sb(f"h0lo{b}", [P, 2, GTOK], F32R) for b in range(2)]
        qT = [sb(f"qT{b}", [P, IC, GTOK]) for b in range(2)]
        kT = [sb(f"kT{b}", [P, IC, 2, GTOK]) for b in range(2)]
        v = [sb(f"v{b}", [P, GT, INNER]) for b in range(2)]
        probs = sb("probs", [P, HEADS, 32])
        smax = sb("smax", [P, HEADS])
        ssum = sb("ssum", [P, HEADS])
        srec = sb("srec", [P, HEADS])
        pT = [sb(f"pT{t}", [P, HEADS, P]) for t in range(GT)]
        oT = [sb(f"oT{t}", [P, IC, P]) for t in range(GT)]
        z = [sb(f"z{t}", [P, D]) for t in range(GT)]
        stats = sb("stats", [P, GT, 6])
        meanvar = sb("meanvar", [P, GT, 2])
        vareps = sb("vareps", [P, GT])
        rstd = sb("rstd", [P, GT])
        x1row = sb("x1row", [P, GT, D + DB])

        p_row = ps("p_row", [P, 512])
        p_qkv = [ps(f"p_qkv{j}", [P, 512]) for j in range(2)]
        p_sc = ps("p_sc", [P, HEADS, 32])
        p_lg = ps("p_lg", [P, 512])
        p_cr = ps("p_cr", [P, 512])
        p_o = ps("p_o", [P, 1024])

        ident = consts[:, C_ID:C_ID + P]
        mask = consts[:, C_MASK:C_MASK + 32]
        half = consts[:, C_HALF:C_HALF + GT]

        s_const = sem("s_const")
        s_x = [sem(f"s_patches{b}") for b in range(2)]
        s_tokw = sem("s_tokw")
        s_wraw = [sem(f"s_wraw_{n}") for n in "qkv"]
        s_graw = sem("s_graw")
        s_gateb = sem("s_gateb")
        s_wo = sem("s_wo")
        s_bo = sem("s_bo")
        s_packh = sem("s_packh")
        s_packl = sem("s_packl")
        s_zero = sem("s_zero")
        s_e = sem("s_e")
        s_row = sem("s_row")
        s_res = sem("s_res")
        s_t0 = sem("s_t0")
        s_hi0 = sem("s_hi0")
        s_lo0 = sem("s_lo0")
        s_qkv = sem("s_qkv")
        s_qevac = sem("s_qevac")
        s_sc = sem("s_sc")
        s_soft = sem("s_soft")
        s_exp = sem("s_exp")
        s_pt = sem("s_pt")
        s_av = sem("s_av")
        s_ot = sem("s_ot")
        s_o = sem("s_o")
        s_ln = sem("s_ln")
        s_ve = sem("s_ve")
        s_rstd = sem("s_rstd")
        s_x1 = sem("s_x1")
        s_acc = sem("s_acc")
        s_t1 = sem("s_t1")
        s_hi1 = sem("s_hi1")
        s_lo1 = sem("s_lo1")
        s_lg = sem("s_lg")
        s_lgc = sem("s_lgc")
        s_lgt = sem("s_lgt")
        s_logit = sem("s_logit")
        s_fb2 = sem("s_fb2")
        s_lnb = sem("s_lnb")
        s_w2 = [sem(f"s_w2{k}") for k in range(2)]
        s_lnbx = sem("s_lnbx")
        s_cr = sem("s_cr")
        s_crep = sem("s_crep")
        s_w1 = sem("s_w1pre")
        s_small = sem("s_small1")

        block = ctx.enter_context(nc.Block())

        @block.sync
        def _(sp):
            def load_x(g, b):
                need(sp, s_e, g - 1)
                for t in range(GT):
                    sp.dma_start(xin[b][:, t, :, :], ins["patches"][bass.ds(g * GT + t, 1), :, :, :]
                                 .rearrange("o p c n -> (o p) c n")).then_inc(s_x[b], 16)

            def load_w2(g):
                need(sp, s_cr, 2 * g)
                for k in range(2):
                    sp.dma_start(w2raw[k][:, :, :], ins["fc2_w"][bass.ds(2 * g + k, 1), :, :, :]
                                 .rearrange("o p c n -> (o p) c n")).then_inc(s_w2[k], 16)

            sp.dma_start(tokw[:, :, :], ins["tok_w"]).then_inc(s_tokw, 16)
            load_x(0, 0)
            sp.dma_start(wraw[0], ins["w_qkv"][0]).then_inc(s_wraw[0], 16)
            sp.dma_start(consts[:, :], ins["consts"]).then_inc(s_const, 16)
            sp.dma_start(wraw[1], ins["w_qkv"][1]).then_inc(s_wraw[1], 16)
            sp.dma_start(wraw[2], ins["w_qkv"][2]).then_inc(s_wraw[2], 16)
            sp.dma_start(bo[:, :], ins["b_o"].to_broadcast([P, D])).then_inc(s_bo, 16)
            sp.dma_start(graw[:, :, :], ins["gate_w"]).then_inc(s_graw, 16)
            load_x(1, 1)
            sp.dma_start(lnb[:, :, :], ins["ln_b"]).then_inc(s_lnb, 16)
            load_w2(0)
            sp.dma_start(wo[:, :, :], ins["w_o"]).then_inc(s_wo, 16)
            sp.dma_start(gateb[:, :], ins["gate_b"].to_broadcast([P, E])).then_inc(s_gateb, 16)
            sp.dma_start(crep[:, :], ins["fc2_b"]).then_inc(s_fb2, 16)
            sp.dma_start(lnw[:, :, :], ins["ln_w"]).then_inc(s_small, 16)
            for k in range(2):
                sp.dma_start(fb1[k][:, :], ins["fc1_b"][k]).then_inc(s_small, 16)
            sp.wait_ge(s_packl, 1)
            sp.dma_start(wbuf[:, :].rearrange("p (e n) -> p e n", e=2),
                         ins["fc1_w"][0:2].rearrange("e p c n -> p e (c n)")).then_inc(s_w1, 16)
            with sp.Fori(1, NG // 2) as turn:
                for b in range(2):
                    load_x(turn * 2 + b, b)
                    load_w2(turn * 2 + b - 1)
            load_w2(NG - 1)
            sp.wait_ge(s_cr, E)
            for k in range(2):
                sp.dma_start(w2raw[k][:, :, :], ins["fc2_w"][k]).then_inc(s_w2[k], 16)
            for k in range(2):
                sp.wait_ge(s_w2[k], 16 * (NG + 1))
            sp.wait_ge(s_small, 16 * 3)

        @block.gpsimd
        def _(pool):
            zeroed = [kT[b][r * H:r * H + H, :, 1 - r, :] for b in range(2) for r in range(2)]
            for k, part in enumerate(zeroed + [pT[t][:, :, :] for t in range(GT)]):
                need(pool, s_zero, k)
                pool.memset(part, 0.0).then_inc(s_zero, 1)
            pool.wait_ge(s_const, 16)

            def norm_group(g):
                held(pool, s_ln, 3 * GT * (g + 1))
                pool.tensor_scalar(vareps[:, :], meanvar[:, :, 1], EPS, None, ALU.add).then_inc(s_ve, 1)
                need(pool, s_ve, g + 1)
                need(pool, s_x1, g)
                pool.tensor_tensor(rstd[:, :], vareps[:, :], half, ALU.pow).then_inc(s_rstd, 1)
                held(pool, s_x1, g + 1)
                pool.tensor_copy(acc[:, bass.ds(g * GT, GT), :], x1row[:, :, 0:D]).then_inc(s_acc, 1)

            def spread(g):
                for k in range(2):
                    need(pool, s_cr, 2 * g + k)
                    pool.tensor_tensor(lnbx[:, :, :],
                                       lnb[:, bass.ds(2 * g + k, 1), :].rearrange("p o c -> p (o c)")
                                       .unsqueeze(2).to_broadcast([P, FC, P]),
                                       consts[:, bass.ds(C_EYE + E - 2 * g - k, P)].unsqueeze(1)
                                       .to_broadcast([P, FC, P]), ALU.mult).then_inc(s_lnbx, 1)

            pool.wait_ge(s_lnb, 16)
            spread(0)
            norm_group(0)
            with pool.Fori(1, NG) as g:
                spread(g)
                norm_group(g)

        @block.scalar
        def _(act):
            def copy_row(g):
                need(act, s_e, g + 1)
                need(act, s_t0, g)
                need(act, s_res, g)
                rows = p_row[:, 0:GT * D].rearrange("p (t d) -> p t d", t=GT)
                act.copy(h0row[:, :, 0:D], rows)
                act.copy(h0row[:, :, D:D + DB], rows[:, :, P:D]).then_inc(s_row, 1)

            def high0(g, b):
                need(act, s_t0, g + 1)
                act.copy(h0hi[b][:, :, :], p_row[:, :].rearrange("p (c n) -> p c n", c=2)).then_inc(s_hi0, 1)

            def high1(g):
                need(act, s_t1, g + 1)
                act.copy(XH[:, :, bass.ds(g * GTOK, GTOK)],
                         p_row[:, :].rearrange("p (c n) -> p c n", c=2)).then_inc(s_hi1, 1)

            def copy_qkv(g, b, item):
                need(act, s_qkv, ITEMS * g + item + 1)
                bank = p_qkv[item % 2]
                if item < IC // 2:
                    act.copy(qT[b][:, 2 * item:2 * item + 2, :], bank[:, :].rearrange("p (c n) -> p c n", c=2)) \
                       .then_inc(s_qevac, 1)
                elif item < IC:
                    c = 2 * (item - IC // 2)
                    for r in range(2):
                        act.copy(kT[b][r * H:r * H + H, c:c + 2, r, :],
                                 bank[r * H:r * H + H, :].rearrange("p (c n) -> p c n", c=2)) \
                           .then_inc(s_qevac, 1)
                else:
                    t, part = (item - IC) // 2, (item - IC) % 2
                    act.copy(v[b][:, t, part * F:part * F + F], bank[:, 0:F]).then_inc(s_qevac, 1)

            def exps(g, t):
                need(act, s_soft, 6 * (GT * g + t) + 3)
                act.activation(probs[:, :, :], probs[:, :, :], ACT.Exp).then_inc(s_exp, 1)

            def copy_ot(g, t):
                need(act, s_av, GT * g + t + 1)
                act.copy(oT[t][:, :, :], p_o[:, 0:INNER].rearrange("p (c n) -> p c n", c=IC)).then_inc(s_ot, 1)

            def copy_logits(g):
                need(act, s_lg, g + 1)
                need(act, s_lgt, g)
                act.copy(logitT[:, :], p_lg[0:E, 0:GTOK]).then_inc(s_lgc, 1)

            copy_row(0)
            high0(0, 0)
            act.wait_ge(s_zero, 4 + GT)
            for item in range(ITEMS):
                copy_qkv(0, 0, item)

            def body(g, b):
                nxt = not (isinstance(g, int) and g == NG - 1)
                if nxt:
                    copy_row(g + 1)
                    high0(g + 1, 1 - b)
                exps(g, 0)
                if nxt:
                    for item in range(IC // 2):
                        copy_qkv(g + 1, 1 - b, item)
                exps(g, 1)
                copy_ot(g, 0)
                if nxt:
                    for item in range(IC // 2, IC + 2):
                        copy_qkv(g + 1, 1 - b, item)
                copy_ot(g, 1)
                if not (isinstance(g, int) and g == 0):
                    high1(g - 1)
                if nxt:
                    for item in range(IC + 2, ITEMS):
                        copy_qkv(g + 1, 1 - b, item)
                if not (isinstance(g, int) and g == 0):
                    copy_logits(g - 1)

            pairs(act, NG, body)
            high1(NG - 1)
            copy_logits(NG - 1)

        @block.vector
        def _(dve):
            def residual(g):
                need(dve, s_row, g + 1)
                dve.tensor_tensor(acc[:, bass.ds(g * GT, GT), :], h0row[:, :, 0:D],
                                  bo[:, :].unsqueeze(1).to_broadcast([P, GT, D]), ALU.add).then_inc(s_res, 1)

            def low0(g, b):
                need(dve, s_hi0, g + 1)
                dve.tensor_tensor(h0lo[b][:, :, :], p_row[:, :].rearrange("p (c n) -> p c n", c=2),
                                  h0hi[b][:, :, :].bitcast(F32), ALU.subtract).then_inc(s_lo0, 1)

            def low1(g):
                need(dve, s_hi1, g + 1)
                cols = bass.ds(g * GTOK, GTOK)
                dve.tensor_tensor(XL[:, :, cols], p_row[:, :].rearrange("p (c n) -> p c n", c=2),
                                  XH[:, :, cols].bitcast(F32), ALU.subtract).then_inc(s_lo1, 1)

            def shift(g, t):
                n = GT * g + t
                need(dve, s_sc, n + 1)
                need(dve, s_pt, n)
                dve.scalar_tensor_tensor(out=probs[:, :, :], in0=p_sc[:, :, :], scalar=SCALE,
                                         in1=mask.unsqueeze(1).to_broadcast([P, HEADS, 32]),
                                         op0=ALU.mult, op1=ALU.add).then_inc(s_soft, 1)
                need(dve, s_soft, 6 * n + 1)
                dve.tensor_reduce(smax[:, :], probs[:, :, :], AX.X, ALU.max).then_inc(s_soft, 1)
                need(dve, s_soft, 6 * n + 2)
                dve.tensor_tensor(probs[:, :, :], probs[:, :, :],
                                  smax[:, :].unsqueeze(2).to_broadcast([P, HEADS, 32]), ALU.subtract) \
                   .then_inc(s_soft, 1)

            def normalise(g, t):
                n = GT * g + t
                need(dve, s_exp, n + 1)
                dve.tensor_reduce(ssum[:, :], probs[:, :, :], AX.X, ALU.add).then_inc(s_soft, 1)
                need(dve, s_soft, 6 * n + 4)
                dve.reciprocal(srec[:, :], ssum[:, :]).then_inc(s_soft, 1)
                need(dve, s_soft, 6 * n + 5)
                dve.tensor_tensor(probs[:, :, :], probs[:, :, :],
                                  srec[:, :].unsqueeze(2).to_broadcast([P, HEADS, 32]), ALU.mult) \
                   .then_inc(s_soft, 1)
                need(dve, s_soft, 6 * n + 6)
                need(dve, s_av, n - 1)
                for q in range(4):
                    rows = slice(32 * q, 32 * q + 32)
                    last = dve.transpose(pT[t][rows, :, 32 * q:32 * q + 32], probs[rows, :, :])
                last.then_inc(s_pt, 1)

            def add_residual(g, t):
                n = GT * g + t
                need(dve, s_o, n + 1)
                dve.tensor_tensor(z[t][:, :], p_o[:, 0:D],
                                  acc[:, bass.ds(g * GT + t, 1), :].rearrange("p o d -> p (o d)"), ALU.add) \
                   .then_inc(s_ln, 1)
                need(dve, s_ln, 3 * n + 1)
                dve.bn_stats(stats[:, t, :], z[t][:, :]).then_inc(s_ln, 1)
                held(dve, s_ln, 3 * n + 2)
                dve.bn_aggr(meanvar[:, t, :], stats[:, t, :]).then_inc(s_ln, 1)

            def norm_rows(g):
                need(dve, s_rstd, g + 1)
                need(dve, s_t1, g)
                need(dve, s_acc, g)
                for t in range(GT):
                    for cols, part in ((slice(0, D), z[t][:, :]), (slice(D, D + DB), z[t][:, P:D])):
                        last = dve.tensor_scalar(x1row[:, t, cols], part, meanvar[:, t, 0:1], rstd[:, t:t + 1],
                                                 ALU.subtract, ALU.mult)
                last.then_inc(s_x1, 1)

            def add_gate(g):
                need(dve, s_lgt, g + 1)
                dve.tensor_tensor(logit[:, bass.ds(g * GT, GT), :],
                                  p_lg[:, GTOK:GTOK + GT * E].rearrange("p (t e) -> p t e", t=GT),
                                  gateb[:, :].unsqueeze(1).to_broadcast([P, GT, E]), ALU.add) \
                   .then_inc(s_logit, 1)

            for j in range(3):
                w = wqkv[:, :, j * INNER:(j + 1) * INNER]
                dve.wait_ge(s_wraw[j], 16)
                pack_high(dve, w, wraw[j]).then_inc(s_packh, 1)
                if j == 1:
                    low0(0, 0)
                dve.wait_ge(s_packh, j + 1)
                pack_low(dve, w, wraw[j]).then_inc(s_packl, 1)
            dve.wait_ge(s_const, 16)
            dve.wait_ge(s_bo, 16)
            residual(0)
            dve.wait_ge(s_graw, 16)
            pack_high(dve, gate_pack, graw).then_inc(s_packh, 1)
            dve.wait_ge(s_packh, 4)
            pack_low(dve, gate_pack, graw).then_inc(s_packl, 1)
            dve.wait_ge(s_gateb, 16)
            dve.wait_ge(s_zero, 4 + GT)

            def body(g, b):
                nxt = not (isinstance(g, int) and g == NG - 1)
                if nxt:
                    residual(g + 1)
                if not (isinstance(g, int) and g <= 1):
                    add_gate(g - 2)
                shift(g, 0)
                if nxt:
                    low0(g + 1, 1 - b)
                normalise(g, 0)
                shift(g, 1)
                normalise(g, 1)
                if not nxt:
                    dve.wait_ge(s_w1, 16)
                    w1raw0 = wbuf[:, 0:2 * F].rearrange("p (c n) -> p c n", c=2)
                    pack_high(dve, w1p0, w1raw0).then_inc(s_packh, 1)
                    dve.wait_ge(s_packh, 5)
                    pack_low(dve, w1p0, w1raw0).then_inc(s_packl, 1)
                add_residual(g, 0)
                if not (isinstance(g, int) and g == 0):
                    low1(g - 1)
                add_residual(g, 1)
                norm_rows(g)

            pairs(dve, NG, body)
            add_gate(NG - 2)
            dve.wait_ge(s_fb2, 16)
            dve.wait_ge(s_cr, E)
            dve.tensor_tensor(crep[:, :], p_cr[:, 0:D], crep[:, :], ALU.add).then_inc(s_crep, 1)
            low1(NG - 1)
            add_gate(NG - 1)

        @block.tensor
        def _(pe):
            def embed(g, b):
                need(pe, s_x[b], 16 * GT * ((g - b) // 2 + 1))
                need(pe, s_hi0, g)
                need(pe, s_lo0, g)
                if not isinstance(g, int) or g >= 3:
                    pe.wait_ge(s_hi1, g - 2)
                    pe.wait_ge(s_lo1, g - 2)
                for t in range(GT):
                    for c in range(KC):
                        mm = pe.matmul(p_row[:, t * D:t * D + D], xin[b][:, t, c, :], tokw[:, c, :],
                                       start=(c == 0), stop=(c == KC - 1))
                mm.then_inc(s_e, 1)

            def turn_rows(rows):
                for c in range(2):
                    for t in range(GT):
                        mm = pe.transpose(p_row[:, (c * GT + t) * P:(c * GT + t + 1) * P],
                                          rows[:, t, c * P:(c + 1) * P], ident)
                return mm

            def transpose0(g):
                need(pe, s_row, g + 1)
                turn_rows(h0row).then_inc(s_t0, 1)

            def transpose1(g):
                need(pe, s_x1, g + 1)
                after = min(g + 3, NG) if isinstance(g, int) else g + 3
                need(pe, s_hi0, after)
                need(pe, s_lo0, after)
                need(pe, s_hi1, g)
                need(pe, s_lo1, g)
                turn_rows(x1row).then_inc(s_t1, 1)

            def qkv(g, b, item):
                if item == 0:
                    need(pe, s_hi0, g + 1)
                    need(pe, s_lo0, g + 1)
                done = [1, 2, 3, 5, 7, 9, 10, 11, 12, 13][(item - 2) % ITEMS]
                need(pe, s_qevac, EVACS * (g if item >= 2 else g - 1) + done)
                bank = p_qkv[item % 2]
                xh, xl = h0hi[b], h0lo[b]
                if item < IC:
                    for j in range(2):
                        c = 2 * item + j
                        terms = stack_terms(wqkv[:, :, c * P:(c + 1) * P], xh, xl)
                        for k, (w, x) in enumerate(terms):
                            mm = pe.matmul(bank[:, j * GTOK:(j + 1) * GTOK], w, x,
                                           start=(k == 0), stop=(k == len(terms) - 1))
                else:
                    t, part = (item - IC) // 2, (item - IC) % 2
                    col = 2 * INNER + part * F
                    cols = slice(t * P, t * P + P)
                    terms = stack_terms(wqkv[:, :, col:col + F], xh[:, :, cols], xl[:, :, cols])
                    for k, (w, x) in enumerate(terms):
                        mm = pe.matmul(bank[:, 0:F], x, w, start=(k == 0), stop=(k == len(terms) - 1))
                mm.then_inc(s_qkv, 1)

            def score(g, b, t):
                need(pe, s_qevac, EVACS * g + 3 * (IC // 2))
                need(pe, s_soft, 6 * (GT * g + t - 1) + 1)
                for c in range(IC):
                    for q in range(4):
                        cols = slice(t * P + 32 * q, t * P + 32 * q + 32)
                        mm = pe.matmul(p_sc[32 * q:32 * q + 32, 2 * c:2 * c + 2, :], qT[b][:, c, cols],
                                       kT[b][:, c, :, cols], start=True, stop=True)
                mm.then_inc(s_sc, 1)

            def attend(g, b, t):
                n = GT * g + t
                need(pe, s_qevac, EVACS * (g + 1))
                need(pe, s_pt, n + 1)
                need(pe, s_ln, 3 * (n - 1) + 1)
                for h in range(HEADS):
                    r = (h % 2) * H
                    mm = pe.matmul(p_o[r:r + H, (h // 2) * P:(h // 2 + 1) * P], v[b][:, t, h * DH:(h + 1) * DH],
                                   pT[t][:, h, :], start=True, stop=True)
                mm.then_inc(s_av, 1)

            def project(g, t):
                need(pe, s_ot, GT * g + t + 1)
                for c in range(IC):
                    mm = pe.matmul(p_o[:, 0:D], oT[t][:, c, :], wo[:, c, :], start=(c == 0), stop=(c == IC - 1))
                mm.then_inc(s_o, 1)

            def router(g):
                need(pe, s_hi1, g + 1)
                need(pe, s_lo1, g + 1)
                need(pe, s_logit, g)
                cols = bass.ds(g * GTOK, GTOK)
                terms = stack_terms(gate_pack, XH[:, :, cols], XL[:, :, cols])
                for k, (w, x) in enumerate(terms):
                    mm = pe.matmul(p_lg[0:E, 0:GTOK], w, x, start=(k == 0), stop=(k == len(terms) - 1))
                mm.then_inc(s_lg, 1)

            def turn_logits(g):
                held(pe, s_lgc, g + 1)
                for t in range(GT):
                    mm = pe.transpose(p_lg[:, GTOK + t * E:GTOK + (t + 1) * E], logitT[:, t * P:(t + 1) * P],
                                      ident[0:E, 0:E])
                mm.then_inc(s_lgt, 1)

            def constant_rows(g, k):
                need(pe, s_lnbx, 2 * g + k + 1)
                need(pe, s_w2[k], 16 * (g + 1))
                first, last = (isinstance(g, int) and g == n and k == m for n, m in ((0, 0), (NG - 1, 1)))
                for f in range(FC):
                    mm = pe.matmul(p_cr[:, 0:D], lnbx[:, f, :], w2raw[k][:, f, :],
                                   start=(first and f == 0), stop=(last and f == FC - 1),
                                   skip_group_check=True)
                mm.then_inc(s_cr, 1)

            pe.wait_ge(s_tokw, 16)
            pe.wait_ge(s_const, 16)
            embed(0, 0)
            transpose0(0)
            for item in range(ITEMS):
                pe.wait_ge(s_packl, min(3, 1 + item // (IC // 2)))
                qkv(0, 0, item)
            pe.wait_ge(s_zero, 4 + GT)
            pe.wait_ge(s_wo, 16)

            def body(g, b):
                nxt = not (isinstance(g, int) and g == NG - 1)
                if nxt:
                    embed(g + 1, 1 - b)
                if not (isinstance(g, int) and g <= 1):
                    turn_logits(g - 2)
                score(g, b, 0)
                constant_rows(g, 0)
                if nxt:
                    transpose0(g + 1)
                score(g, b, 1)
                constant_rows(g, 1)
                if nxt:
                    for item in range(IC // 2):
                        qkv(g + 1, 1 - b, item)
                attend(g, b, 0)
                if nxt:
                    for item in range(IC // 2, IC):
                        qkv(g + 1, 1 - b, item)
                project(g, 0)
                if nxt:
                    for item in range(IC, IC + 2):
                        qkv(g + 1, 1 - b, item)
                attend(g, b, 1)
                if not (isinstance(g, int) and g == 0):
                    transpose1(g - 1)
                if nxt:
                    qkv(g + 1, 1 - b, IC + 2)
                project(g, 1)
                if nxt:
                    qkv(g + 1, 1 - b, IC + 3)
                if not (isinstance(g, int) and g == 0):
                    router(g - 1)

            pairs(pe, NG, body)
            turn_logits(NG - 2)
            transpose1(NG - 1)
            router(NG - 1)
            turn_logits(NG - 1)


def experts(nc, ins, consts, XH, XL, acc, logit, crep, lnw, fb1, wbuf, w1p0, w2raw, out):
    with ExitStack() as ctx:
        def sb(name, shape, dt=F32):
            return ctx.enter_context(nc.sbuf_tensor(name, shape, dt))

        def ps(name, shape):
            return ctx.enter_context(nc.psum_tensor(name, shape, F32))

        def sem(name):
            return ctx.enter_context(nc.semaphore(name))

        w1raw = [wbuf[:, b * 2 * F:(b + 1) * 2 * F].rearrange("p (c n) -> p c n", c=2) for b in range(2)]
        w1p = [w1p0, sb("w1p1", [P, 4, F], F32R)]
        w2s = sb("w2s", [P, FC, D])
        w2c = sb("w2c", [P, FC, D])
        c_hi = [sb(f"c_hi{b}", [P, FC, CW], F32R) for b in range(2)]
        c_lo = [sb(f"c_lo{b}", [P, FC, CW], F32R) for b in range(2)]
        g = [sb(f"g{b}", [P, FC, STOK]) for b in range(2)]
        g_hi = [sb(f"g_hi{b}", [P, FC, STOK], F32R) for b in range(2)]
        g_lo = [sb(f"g_lo{b}", [P, FC, STOK], F32R) for b in range(2)]
        sq = sb("sq", [P, FC, STOK])
        sq01 = sb("sq01", [P, STOK])
        sqsum = [sb(f"sqsum{b}", [P, STOK]) for b in range(2)]
        sqT = sb("sqT", [P, STOK])
        sqq = [sb(f"sqq{b}", [P, STOK // 32]) for b in range(2)]
        sums = [sb(f"sums{b}", [P, ST]) for b in range(2)]
        sqm = sb("sqm", [P, ST, 4])
        sqn = [sb(f"sqn{b}", [P, ST]) for b in range(2)]
        sumg2 = sb("sumg2", [P, ST])
        varn = sb("varn", [P, ST])
        vare = sb("vare", [P, ST])
        rn = sb("rn", [P, ST])
        scale = [sb(f"scale{b}", [P, ST]) for b in range(2)]
        lmax = sb("lmax", [P, NT])
        lsum = sb("lsum", [P, NT])
        lrec = sb("lrec", [P, NT])
        prob = sb("prob", [P, NT, E + 8])
        top8 = sb("top8", [P, NT, 8])
        marked = sb("marked", [P, NT, E + 8])
        comb = sb("comb", [P, NT, E])
        combn = sb("combn", [P, E, NT])
        combT = sb("combT", [P, 2, P])
        crows = sb("crows", [P, 8, D])
        st2 = sb("st2", [P, NT, 6])
        mv2 = sb("mv2", [P, NT, 2])
        ve2 = sb("ve2", [P, NT])
        rs2 = sb("rs2", [P, NT])
        res = sb("res", [P, NT, D])

        p_h = [ps(f"p_h{f}", [P, STOK]) for f in range(FC)]
        p_w = ps("p_w", [P, 512])
        p_y = [ps(f"p_y{b}", [P, ST, YW]) for b in range(2)]

        ident = consts[:, C_ID:C_ID + P]
        ones = consts[:, C_ONES:C_ONES + P]
        rowmask = consts[:, C_ROW:C_ROW + 8]
        half = consts[:, C_HALF:C_HALF + NT]
        quad = consts[:, C_QUAD:C_QUAD + 4]
        fold = consts[:, C_FOLD:C_FOLD + P]

        s_w1 = [sem(f"s_w1raw{b}") for b in range(2)]
        s_b1 = [sem(f"s_b1{b}") for b in range(2)]
        s_w2 = [sem(f"s_w2raw{b}") for b in range(2)]
        s_ph = sem("s_ph")
        s_w1p = sem("s_w1p")
        s_w2s = sem("s_w2s")
        s_mean = sem("s_mean")
        s_cen = sem("s_cen")
        s_chi = sem("s_chi")
        s_cp = sem("s_cp")
        s_pad = sem("s_pad")
        s_r = sem("s_r")
        s_rexp = sem("s_rexp")
        s_crow = sem("s_crow")
        s_combt = sem("s_combt")
        s_combs = sem("s_combs")
        s_init = sem("s_init")
        s_initd = sem("s_initd")
        s_g1 = sem("s_g1")
        s_gelu = sem("s_gelu")
        s_sq = sem("s_sq")
        s_sq01 = sem("s_sq01")
        s_sqs = sem("s_sqs")
        s_sqt = sem("s_sqt")
        s_sqq = sem("s_sqq")
        s_hi = sem("s_hi")
        s_lo = sem("s_lo")
        s_y = sem("s_y")
        s_sums = sem("s_sums")
        s_v = sem("s_v")
        s_scale = sem("s_scale")
        s_ev = sem("s_ev")
        s_f = sem("s_f")
        s_fa = sem("s_fa")
        s_fp = sem("s_fp")
        s_res = sem("s_res2")
        s_out = sem("s_out")

        block = ctx.enter_context(nc.Block())

        @block.sync
        def _(sp):
            def load_bias(e, b):
                need(sp, s_gelu, FC * NQ * (e - 1))
                sp.dma_start(fb1[b][:, :], ins["fc1_b"][bass.ds(e, 1), :, :].rearrange("o p c -> (o p) c")) \
                   .then_inc(s_b1[b], 16)

            def load_weights(e, b):
                need(sp, s_w1p, e - 1)
                sp.dma_start(w1raw[b], ins["fc1_w"][bass.ds(e, 1), :, :, :]
                             .rearrange("o p c n -> (o p) c n")).then_inc(s_w1[b], 16)
                need(sp, s_w2s, e - 1)
                sp.dma_start(w2raw[b][:, :, :], ins["fc2_w"][bass.ds(e, 1), :, :, :]
                             .rearrange("o p c n -> (o p) c n")).then_inc(s_w2[b], 16)
                load_bias(e, b)

            with sp.Fori(1, E // 2) as turn:
                for b in range(2):
                    load_weights(turn * 2 + b, b)
            for t in range(NT):
                sp.wait_ge(s_res, t + 1)
                sp.dma_start(out[t * P:(t + 1) * P, :], res[:, t, :]).then_inc(s_out, 16)
            sp.wait_ge(s_out, 16 * NT)

        @block.gpsimd
        def _(pool):
            def scale_w2(e, b):
                need(pool, s_w2[b], 16 * ((e - b) // 2))
                need(pool, s_cen, e)
                pool.tensor_tensor(w2s[:, :, :], w2raw[b][:, :, :],
                                   lnw[:, bass.ds(e, 1), :].rearrange("p o c -> p (o c)")
                                   .unsqueeze(2).to_broadcast([P, FC, D]), ALU.mult).then_inc(s_w2s, 1)

            def sum_squares(i, b):
                need(pool, s_sq, i + 1)
                need(pool, s_sqs, i)
                pool.tensor_tensor(sq01[:, :], sq[:, 0, :], sq[:, 1, :], ALU.add).then_inc(s_sq01, 1)
                need(pool, s_sq01, i + 1)
                need(pool, s_sqt, i - 1)
                pool.tensor_tensor(sqsum[b][:, :], sq01[:, :], sq[:, 2, :], ALU.add).then_inc(s_sqs, 1)

            def factors(i, b, expert, q):
                need(pool, s_sums, 3 * i + 3)
                pool.tensor_tensor(sumg2[:, :], sums[b][:, :], sums[b][:, :], ALU.mult).then_inc(s_v, 1)
                need(pool, s_v, 4 * i + 1)
                pool.tensor_tensor(varn[:, :], sqn[b][:, :], sumg2[:, :], ALU.subtract).then_inc(s_v, 1)
                held(pool, s_v, 4 * i + 2)
                pool.tensor_scalar(vare[:, :], varn[:, :], 0.0, EPS * F * F, ALU.max, ALU.add).then_inc(s_v, 1)
                need(pool, s_v, 4 * i + 3)
                pool.tensor_tensor(rn[:, :], vare[:, :], half[:, 0:ST], ALU.pow).then_inc(s_v, 1)
                need(pool, s_v, 4 * i + 4)
                need(pool, s_ev, i - 1)
                pool.tensor_tensor(scale[b][:, :], rn[:, :],
                                   combn[:, bass.ds(expert, 1), q * ST:(q + 1) * ST].rearrange("p o t -> p (o t)"),
                                   ALU.mult).then_inc(s_scale, 1)

            def final_deviation(q):
                tiles = slice(q * ST, (q + 1) * ST)
                pool.wait_ge(s_fa, (q + 1) * ST)
                pool.tensor_scalar(ve2[:, tiles], mv2[:, tiles, 1], EPS, None, ALU.add).then_inc(s_fp, 1)
                pool.wait_ge(s_fp, 2 * q + 1)
                pool.tensor_tensor(rs2[:, tiles], ve2[:, tiles], half[:, 0:ST], ALU.pow).then_inc(s_fp, 1)

            scale_w2(0, 0)
            for b in range(2):
                pool.memset(c_hi[b][:, :, D:D + 1].bitcast(F32), 1.0)
                pool.memset(c_hi[b][:, :, D + 1:CW].bitcast(F32), 0.0)
                last = pool.memset(c_lo[b][:, :, D:CW].bitcast(F32), 0.0)
            last.then_inc(s_pad, 1)

            def body(e, b):
                last = isinstance(e, int) and e == E - 1
                for q in range(NQ):
                    i = e * NQ + q
                    sum_squares(i, q % 2)
                    if isinstance(e, int) and i == 1:
                        pool.wait_ge(s_r, R_COMBN)
                    if not (isinstance(e, int) and i == 0):
                        factors(i - 1, (q + 1) % 2, e if q else e - 1, (q - 1) % NQ)
                    if q == 0 and not last:
                        scale_w2(e + 1, 1 - b)
                    if last and q >= 2:
                        final_deviation(q - 2)

            pairs(pool, E, body)
            factors(STEPS - 1, (NQ - 1) % 2, E - 1, NQ - 1)
            for q in (NQ - 2, NQ - 1):
                final_deviation(q)

        @block.scalar
        def _(act):
            def gelus(i, b, e_b):
                for f in range(FC):
                    need(act, s_g1, FC * i + f + 1)
                    need(act, s_lo, FC * (i - 2) + f + 1)
                    if f == 0:
                        need(act, s_sq, i - 1)
                    act.activation(g[b][:, f, :], p_h[f][:, :], ACT.Gelu, bias=fb1[e_b][:, f:f + 1]) \
                       .then_inc(s_gelu, 1)
                    need(act, s_gelu, FC * i + f + 1)
                    if f == 0:
                        need(act, s_y, i - 1)
                    act.copy(g_hi[b][:, f, :], g[b][:, f, :]).then_inc(s_hi, 1)
                need(act, s_sqs, i)
                act.activation(sq[:, :, :], g[b][:, :, :], ACT.Square).then_inc(s_sq, 1)

            act.wait_ge(s_r, 3)
            act.activation(prob[:, :, 0:E], logit[:, :, :], ACT.Exp).then_inc(s_rexp, 1)

            def body(e, b):
                need(act, s_b1[b], 16 * ((e - b) // 2))
                for q in range(NQ):
                    gelus(e * NQ + q, q % 2, b)

            pairs(act, E, body)

        @block.vector
        def _(dve):
            def pack_w1(e, b):
                need(dve, s_w1[b], 16 * ((e - b) // 2))
                need(dve, s_g1, FC * NQ * (e - 1))
                pack_high(dve, w1p[b], w1raw[b]).then_inc(s_ph, 1)
                need(dve, s_ph, e)
                pack_low(dve, w1p[b], w1raw[b]).then_inc(s_w1p, 1)

            def pack_w2(e, b):
                need(dve, s_mean, e + 1)
                dve.scalar_tensor_tensor(out=w2c[:, :, :], in0=p_w[:, 0:D].unsqueeze(1).to_broadcast([P, FC, D]),
                                         scalar=-1.0 / F, in1=w2s[:, :, :], op0=ALU.mult, op1=ALU.add) \
                   .then_inc(s_cen, 1)
                need(dve, s_cen, e + 1)
                need(dve, s_y, NQ * (e - 1))
                dve.tensor_copy(c_hi[b][:, :, 0:D], w2c[:, :, :]).then_inc(s_chi, 1)
                need(dve, s_chi, e + 1)
                dve.tensor_tensor(c_lo[b][:, :, 0:D], w2c[:, :, :], c_hi[b][:, :, 0:D].bitcast(F32),
                                  ALU.subtract).then_inc(s_cp, 1)

            def split(i, b, f):
                need(dve, s_hi, FC * i + f + 1)
                if f == 0:
                    need(dve, s_y, i - 1)
                dve.tensor_tensor(g_lo[b][:, f, :], g[b][:, f, :], g_hi[b][:, f, :].bitcast(F32),
                                  ALU.subtract).then_inc(s_lo, 1)

            def fold_squares(i, b):
                need(dve, s_sqs, i + 1)
                need(dve, s_sqq, i)
                need(dve, s_y, i - 1)
                dve.transpose(sqT[:, :], sqsum[b][:, :]).then_inc(s_sqt, 1)
                need(dve, s_sqt, i + 1)
                dve.tensor_reduce(sqq[b][:, :], sqT[:, :].rearrange("p (n k) -> p n k", k=32), AX.X, ALU.add) \
                   .then_inc(s_sqq, 1)

            def copy_sums(i, b):
                need(dve, s_y, i + 1)
                need(dve, s_v, 4 * (i - 2) + 2)
                dve.tensor_copy(sums[b][:, :], p_y[b][:, :, SUMG]).then_inc(s_sums, 1)
                need(dve, s_sums, 3 * (i - 1) + 3)
                dve.tensor_tensor(sqm[:, :, :], p_y[b][:, 0, SUMSQ:SUMSQ + STOK // 32]
                                  .rearrange("p (t k) -> p t k", k=4),
                                  quad.unsqueeze(1).to_broadcast([P, ST, 4]), ALU.mult).then_inc(s_sums, 1)
                need(dve, s_sums, 3 * i + 2)
                dve.tensor_reduce(sqn[b][:, :], sqm[:, :, :], AX.X, ALU.add).then_inc(s_sums, 1)

            def add_out(i, b, q):
                need(dve, s_scale, i + 1)
                need(dve, s_ev, i - NQ + 1)
                for t in range(ST):
                    tile = acc[:, q * ST + t, :]
                    last = dve.scalar_tensor_tensor(out=tile, in0=p_y[b][:, t, 0:D], scalar=scale[b][:, t:t + 1],
                                                    in1=tile, op0=ALU.mult, op1=ALU.add)
                last.then_inc(s_ev, 1)

            step = [0]

            def r(ins):
                step[0] += 1
                ins.then_inc(s_r, 1)
                dve.wait_ge(s_r, step[0])

            def router_logits():
                dve.memset(prob[:, :, E:E + 8], -1.0)
                r(dve.memset(logit[:, :, 0:SHARED], NEG_INF))
                r(dve.tensor_reduce(lmax[:, :], logit[:, :, :], AX.X, ALU.max))
                r(dve.tensor_tensor(logit[:, :, :], logit[:, :, :],
                                    lmax[:, :].unsqueeze(2).to_broadcast([P, NT, E]), ALU.subtract))

            def router_weights():
                dve.wait_ge(s_rexp, 1)
                r(dve.tensor_reduce(lsum[:, :], prob[:, :, 0:E], AX.X, ALU.add))
                r(dve.reciprocal(lrec[:, :], lsum[:, :]))
                r(dve.tensor_tensor(prob[:, :, 0:E], prob[:, :, 0:E],
                                    lrec[:, :].unsqueeze(2).to_broadcast([P, NT, E]), ALU.mult))
                for t in range(NT):
                    last = dve.max(top8[:, t, :], prob[:, t, :])
                r(last)
                r(dve.memset(top8[:, :, ROUTE:8], -1.0))
                for t in range(NT):
                    last = dve.match_replace(marked[:, t, :], top8[:, t, :], prob[:, t, :], -2.0)
                r(last)
                r(dve.scalar_tensor_tensor(out=comb[:, :, :], in0=marked[:, :, 0:E], scalar=-2.0,
                                           in1=prob[:, :, 0:E], op0=ALU.is_equal, op1=ALU.mult))
                r(dve.tensor_scalar(comb[:, :, 0:SHARED], comb[:, :, 0:SHARED], 1.0, None, ALU.add))
                r(dve.tensor_scalar(combn[:, :, :].rearrange("p e t -> p t e"), comb[:, :, :], float(F), None,
                                    ALU.mult))
                assert step[0] == R_COMBN

            def mask_rows():
                dve.tensor_tensor(crows[:, :, :], crep[:, :].unsqueeze(1).to_broadcast([P, 8, D]),
                                  rowmask.unsqueeze(2).to_broadcast([P, 8, D]), ALU.mult).then_inc(s_crow, 1)

            def copy_comb():
                dve.wait_ge(s_combt, 1)
                dve.tensor_copy(combT[:, :, :], p_w[:, 0:2 * P].rearrange("p (c n) -> p c n", c=2)) \
                   .then_inc(s_combs, 1)

            def add_constant(j):
                dve.wait_ge(s_init, j + 1)
                dve.tensor_tensor(acc[:, 2 * j:2 * j + 2, :], p_w[:, 0:2 * D].rearrange("p (t d) -> p t d", t=2),
                                  acc[:, 2 * j:2 * j + 2, :], ALU.add).then_inc(s_initd, 1)

            def final_stats(q):
                dve.wait_ge(s_ev, STEPS - NQ + q + 1)
                for t in range(q * ST, (q + 1) * ST):
                    dve.bn_stats(st2[:, t, :], acc[:, t, :]).then_inc(s_f, 1)
                for t in range(q * ST, (q + 1) * ST):
                    dve.wait_ge(s_f, 1 + t)
                    dve.bn_aggr(mv2[:, t, :], st2[:, t, :]).then_inc(s_fa, 1)

            def final_norm(q):
                dve.wait_ge(s_fp, 2 * q + 2)
                for t in range(q * ST, (q + 1) * ST):
                    dve.tensor_scalar(res[:, t, :], acc[:, t, :], mv2[:, t, 0:1], rs2[:, t:t + 1],
                                      ALU.subtract, ALU.mult).then_inc(s_res, 1)

            router_logits()
            dve.wait_ge(s_pad, 1)
            pack_w2(0, 0)
            for f in range(FC):
                split(0, 0, f)

            def body(e, b):
                last = isinstance(e, int) and e == E - 1
                first = isinstance(e, int) and e == 0
                for q in range(NQ):
                    i = e * NQ + q
                    constants = isinstance(e, int) and (e, q) in CONSTANT_AT
                    more = not (last and q == NQ - 1)
                    if not (first and q == 0):
                        copy_sums(i - 1, (q + 1) % 2)
                    if first and q == NQ - 1:
                        copy_comb()
                    if constants:
                        add_constant(2 * CONSTANT_AT.index((e, q)))
                    if more:
                        split(i + 1, (q + 1) % 2, 0)
                    fold_squares(i, q % 2)
                    if more:
                        split(i + 1, (q + 1) % 2, 1)
                        split(i + 1, (q + 1) % 2, 2)
                    if constants:
                        add_constant(2 * CONSTANT_AT.index((e, q)) + 1)
                    if first and q == 0:
                        router_weights()
                        mask_rows()
                    else:
                        add_out(i - 1, (q + 1) % 2, (q - 1) % NQ)
                    if q == 0 and not last:
                        pack_w1(e + 1, 1 - b)
                    if q == (1 if isinstance(e, int) and e <= 1 else 2) and not last:
                        pack_w2(e + 1, 1 - b)
                    if last and q >= 1:
                        final_stats(q - 1)
                    if last and q >= 2:
                        final_norm(q - 2)

            pairs(dve, E, body)
            copy_sums(STEPS - 1, (NQ - 1) % 2)
            add_out(STEPS - 1, (NQ - 1) % 2, NQ - 1)
            final_stats(NQ - 1)
            for q in (NQ - 2, NQ - 1):
                final_norm(q)

        @block.tensor
        def _(pe):
            def hidden(i, b, q):
                cols = slice(q * STOK, (q + 1) * STOK)
                for f in range(FC):
                    need(pe, s_gelu, FC * (i - 1) + f + 1)
                    terms = stack_terms(w1p[b][:, :, f * P:(f + 1) * P], XH[:, :, cols], XL[:, :, cols])
                    for k, (w, x) in enumerate(terms):
                        mm = pe.matmul(p_h[f][:, :], w, x, start=(k == 0), stop=(k == len(terms) - 1))
                    mm.then_inc(s_g1, 1)

            def outputs(i, b, par):
                need(pe, s_lo, FC * (i + 1))
                need(pe, s_ev, i - 1)
                for t in (2, 3, 0, 1):
                    cols = slice(t * P, t * P + P)
                    for f in range(FC):
                        for k, (gx, wx) in enumerate(((g_hi, c_hi), (g_hi, c_lo), (g_lo, c_hi))):
                            pe.matmul(p_y[par][:, t, 0:CW], gx[par][:, f, cols], wx[b][:, f, :],
                                      start=(t % 2 == 0 and f == 0 and k == 0), stop=(f == FC - 1 and k == 2),
                                      skip_group_check=True)
                need(pe, s_sqq, i + 1)
                pe.matmul(p_y[par][:, 0, SUMSQ:SUMSQ + STOK // 32], fold, sqq[par][:, :],
                          start=False, stop=True, skip_group_check=True).then_inc(s_y, 1)

            def column_sums(e):
                need(pe, s_w2s, e + 1)
                need(pe, s_cen, e)
                if not (isinstance(e, int) and e <= 1):
                    pe.wait_ge(s_initd, NT // 4 if isinstance(e, int) and e == 2 else NT // 2)
                for f in range(FC):
                    mm = pe.matmul(p_w[:, 0:D], ones, w2s[:, f, :], start=(f == 0), stop=(f == FC - 1))
                mm.then_inc(s_mean, 1)

            def turn_comb():
                pe.wait_ge(s_r, R_COMBN)
                pe.wait_ge(s_cen, 2)
                for j in range(2):
                    mm = pe.transpose(p_w[:, j * P:(j + 1) * P],
                                      comb[:, 8 * j:8 * j + 8, :].rearrange("p t e -> p (t e)"), ident)
                mm.then_inc(s_combt, 1)

            def constant(j):
                pe.wait_ge(s_crow, 1)
                pe.wait_ge(s_combs, 1)
                need(pe, s_initd, j)
                pe.wait_ge(s_cen, 3 if j >= NT // 4 else 2)
                for t in (2 * j, 2 * j + 1):
                    mm = pe.matmul(p_w[:, (t % 2) * D:(t % 2 + 1) * D], combT[:, t // 8, :], crows[:, t % 8, :],
                                   start=True, stop=True)
                mm.then_inc(s_init, 1)

            hidden(0, 0, 0)
            column_sums(0)

            def body(e, b):
                last = isinstance(e, int) and e == E - 1
                for q in range(NQ):
                    i = e * NQ + q
                    if isinstance(e, int) and (e, q) in CONSTANT_AT:
                        constant(2 * CONSTANT_AT.index((e, q)))
                    if q < NQ - 1:
                        hidden(i + 1, b, q + 1)
                    elif not last:
                        need(pe, s_w1p, e + 1)
                        hidden(i + 1, 1 - b, 0)
                    if isinstance(e, int) and (e, q) in CONSTANT_AT:
                        constant(2 * CONSTANT_AT.index((e, q)) + 1)
                    if q == 1 and not last:
                        column_sums(e + 1)
                    if q == 0:
                        need(pe, s_cp, e + 1)
                    outputs(i, b, q % 2)
                    if isinstance(e, int) and (e, q) == (0, 2):
                        turn_comb()

            pairs(pe, E, body)


R_COMBN = 12
CONSTANT_AT = [(0, 3), (1, 0), (1, 2), (1, 3)]


def vit_layer(nc, ins, out):
    with ExitStack() as ctx:
        def sb(name, shape, dt=F32):
            return ctx.enter_context(nc.sbuf_tensor(name, shape, dt))

        consts = sb("consts", [P, C_END])
        gate_pack = sb("gate_pack", [P, 4, E], F32R)
        XH = sb("XH", [P, 2, TOK], F32R)
        XL = sb("XL", [P, 2, TOK], F32R)
        acc = sb("acc", [P, NT, D])
        logit = sb("logit", [P, NT, E])
        crep = sb("crep", [P, D])
        lnb = sb("lnb", [P, E, FC])
        lnw = sb("lnw", [P, E, FC])
        fb1 = [sb(f"fb1{b}", [P, FC]) for b in range(2)]
        wbuf = sb("wbuf", [P, 4 * F])
        w1p0 = sb("w1p0", [P, 4, F], F32R)
        w2raw = [sb(f"w2raw{k}", [P, FC, D]) for k in range(2)]
        attention(nc, ins, consts, gate_pack, XH, XL, acc, logit, crep, lnb, lnw, fb1, wbuf, w1p0, w2raw)
        experts(nc, ins, consts, XH, XL, acc, logit, crep, lnw, fb1, wbuf, w1p0, w2raw, out)


def kernel(**inputs):
    import numpy as np
    import concourse.bacc as bacc
    from concourse.bass_utils import run_bass_kernel_spmd

    a = {k: np.asarray(x) for k, x in inputs.items()}

    def doubled(w):
        return np.stack([w[:P], np.concatenate([w[P:], w[P:]])], axis=1)

    def by_chunk(w, c):
        return w.reshape(c, P, -1).transpose(1, 0, 2)

    x = a["x"].reshape(IMAGES, CHANNELS, SIDE // PATCH, PATCH, SIDE // PATCH, PATCH)
    x = x.transpose(3, 5, 1, 0, 2, 4).reshape(KC, P, NT, P).transpose(2, 1, 0, 3)
    consts = np.zeros((P, C_END), np.float32)
    consts[:, C_ID:C_ID + P] = np.eye(P)
    rows = np.arange(P)
    other = (rows[:, None] % 32) // SEQ != np.arange(32)[None, :] // SEQ
    consts[:, C_MASK:C_MASK + 32][other] = MASKED
    consts[:, C_ONES:C_ONES + P] = 1.0
    consts[:, C_ROW:C_ROW + 8] = rows[:, None] // E == np.arange(8)[None, :]
    consts[:, C_HALF:C_QUAD] = -0.5
    consts[:, C_QUAD:C_FOLD] = F * (rows[:, None] // 32 == np.arange(4)[None, :])
    consts[:, C_FOLD:C_END] = rows[:, None] % 32 == rows[None, :] % 32
    consts[:, C_EYE:C_EYE + P + E:E] = 1.0
    arrays = {
        "consts": consts,
        "patches": x,
        "tok_w": by_chunk(a["L0_tok_W"], KC),
        "w_qkv": np.stack([doubled(a[f"L0_attn_w_{n}"]) for n in "qkv"]),
        "w_o": by_chunk(a["L0_attn_w_o"], IC),
        "b_o": a["L0_attn_b_o"].reshape(1, D),
        "gate_w": doubled(a["L0_ffn_gate_w"]),
        "gate_b": a["L0_ffn_gate_b"].reshape(1, E),
        "fc1_w": np.stack([doubled(w) for w in a["L0_ffn_fc1_w"]]),
        "fc1_b": a["L0_ffn_fc1_b"].reshape(E, FC, P).transpose(0, 2, 1),
        "ln_w": a["L0_ffn_ln_w"].reshape(E, FC, P).transpose(2, 0, 1),
        "ln_b": a["L0_ffn_ln_b"].reshape(E, FC, P).transpose(2, 0, 1),
        "fc2_w": a["L0_ffn_fc2_w"].reshape(E, FC, P, D).transpose(0, 2, 1, 3),
        "fc2_b": np.concatenate([a["L0_ffn_fc2_b"]] * 8),
    }
    arrays = {k: np.ascontiguousarray(w) for k, w in arrays.items()}
    nc = bacc.Bacc("TRN2", target_bir_lowering=False, num_devices=1)
    ins = {k: nc.dram_tensor(f"in_{k}", w.shape, F32, kind="ExternalInput").ap() for k, w in arrays.items()}
    out = nc.dram_tensor("out_0", (IMAGES, SEQ, D), F32, kind="ExternalOutput").ap()
    vit_layer(nc, ins, out.rearrange("b n d -> (b n) d"))
    r = run_bass_kernel_spmd(nc, [{f"in_{k}": w for k, w in arrays.items()}], core_ids=[0])
    return r.results[0]["out_0"]
```

```python
from contextlib import ExitStack

import concourse.bass as bass
from concourse import mybir

F32 = mybir.dt.float32
F32R = mybir.dt.float32r
ALU = mybir.AluOpType
ACT = mybir.ActivationFunctionType
AX = mybir.AxisListType

P = 128
H = 64
PATCH = 16
IMAGES, CHANNELS, SIDE = 128, 3, 64
SEQ = (SIDE // PATCH) ** 2
TOK = IMAGES * SEQ
NT = TOK // P
KC = CHANNELS * PATCH * PATCH // P
D = 192
DB = D - P
HEADS, DH = 12, 64
INNER = HEADS * DH
IC = INNER // P
SCALE = 1.0 / 8.0
MASKED = -1e30
E = 16
F = 384
FC = F // P
SHARED, ROUTE = 1, 3
NEG_INF = -1e9
EPS = 1e-5

GT = 2
GTOK = GT * P
NG = NT // GT
ST = 4
STOK = ST * P
NQ = NT // ST
STEPS = E * NQ
YW = 256
CW = D + 2
SUMG, SUMSQ = D, D + 2
ITEMS = 2 * (IC // 2) + 2 * GT
EVACS = IC // 2 + 2 * (IC // 2) + 2 * GT

C_ID, C_MASK, C_ONES, C_EYE, C_ROW, C_HALF, C_QUAD, C_FOLD, C_END = 0, 128, 160, 288, 432, 440, 456, 464, 592


def need(eng, sem, count):
    if not (isinstance(count, int) and count <= 0):
        eng.wait_ge(sem, count)


def held(eng, sem, count):
    need(eng, sem, count)
    eng.nop(nofuse=True)


def pairs(eng, n, body):
    for k in (0, 1):
        body(k, k)
    with eng.Fori(1, n // 2 - 1) as turn:
        for k in (0, 1):
            body(turn * 2 + k, k)
    for k in (n - 2, n - 1):
        body(k, k % 2)


def stack_terms(w, xh, xl):
    return [(w[:, 0, :], xh[:, 0, :]), (w[:, 0, :], xl[:, 0, :]), (w[:, 1, :], xh[:, 0, :]),
            (w[:, 2, :], xh[:, 1, :]), (w[:, 3, :], xl[:, 1, :])]


def pack_high(dve, w, raw):
    dve.tensor_copy(w[:, 0, :], raw[:, 0, :])
    dve.tensor_copy(w[0:H, 2, :], raw[0:H, 1, :])
    return dve.tensor_copy(w[H:P, 3, :], raw[H:P, 1, :])


def pack_low(dve, w, raw):
    dve.tensor_tensor(w[:, 1, :], raw[:, 0, :], w[:, 0, :].bitcast(F32), ALU.subtract)
    dve.tensor_tensor(w[H:P, 2, :], raw[H:P, 1, :], w[H:P, 3, :].bitcast(F32), ALU.subtract)
    return dve.tensor_tensor(w[0:H, 3, :], raw[0:H, 1, :], w[0:H, 2, :].bitcast(F32), ALU.subtract)


def hidden_chunk(pe, bank, w1p, XH, XL, f, q):
    cols = slice(q * STOK, (q + 1) * STOK)
    terms = stack_terms(w1p[:, :, f * P:(f + 1) * P], XH[:, :, cols], XL[:, :, cols])
    for k, (w, x) in enumerate(terms):
        mm = pe.matmul(bank[:, :], w, x, start=(k == 0), stop=(k == len(terms) - 1))
    return mm


def attention(nc, ins, consts, gate_pack, XH, XL, acc, logit, crep, lnb, lnw, fb1, wbuf, w1p0, w2raw, p_h, s_g1):
    with ExitStack() as ctx:
        def sb(name, shape, dt=F32):
            return ctx.enter_context(nc.sbuf_tensor(name, shape, dt))

        def ps(name, shape):
            return ctx.enter_context(nc.psum_tensor(name, shape, F32))

        def sem(name):
            return ctx.enter_context(nc.semaphore(name))

        xin = [sb(f"xin{b}", [P, GT, KC, P]) for b in range(2)]
        tokw = sb("tokw", [P, KC, D])
        wraw = [wbuf[:, :].rearrange("p (c n) -> p c n", c=2)] + \
            [acc[:, j * NT // 2:(j + 1) * NT // 2, :].rearrange("p t d -> p (t d)").rearrange("p (c n) -> p c n", c=2)
             for j in range(2)]
        strip = [sb(f"strip{k}", [P, P]) for k in range(2)]
        logitT = sb("logitT", [E, GTOK])
        gateb = sb("gateb", [P, E])
        graw = sb("graw", [P, 2, E])
        wqkv = sb("wqkv", [P, 4, 3 * INNER], F32R)
        wo = sb("wo", [P, IC, D])
        bo = sb("bo", [P, D])
        h0row = sb("h0row", [P, GT, D + DB])
        h0hi = [sb(f"h0hi{b}", [P, 2, GTOK], F32R) for b in range(2)]
        h0lo = [sb(f"h0lo{b}", [P, 2, GTOK], F32R) for b in range(2)]
        qT = [sb(f"qT{b}", [P, IC, GTOK]) for b in range(2)]
        kT = [sb(f"kT{b}", [P, IC, 2, GTOK]) for b in range(2)]
        v = [sb(f"v{b}", [P, GT, INNER]) for b in range(2)]
        probs = sb("probs", [P, HEADS, 32])
        smax = sb("smax", [P, HEADS])
        ssum = sb("ssum", [P, HEADS])
        srec = sb("srec", [P, HEADS])
        pT = [sb(f"pT{t}", [P, HEADS, P]) for t in range(GT)]
        oT = [sb(f"oT{t}", [P, IC, P]) for t in range(GT)]
        z = [sb(f"z{t}", [P, D]) for t in range(GT)]
        stats = sb("stats", [P, GT, 6])
        meanvar = sb("meanvar", [P, GT, 2])
        vareps = sb("vareps", [P, GT])
        rstd = sb("rstd", [P, GT])
        x1row = sb("x1row", [P, GT, D + DB])

        p_row = ps("p_row", [P, 512])
        p_qkv = p_h[0:2]
        p_sc = p_h[2][:, 0:HEADS * 32].rearrange("p (h n) -> p h n", h=HEADS)
        p_lg = ps("p_lg", [P, 512])
        p_cr = ps("p_cr", [P, 512])
        p_o = ps("p_o", [P, 1024])

        ident = consts[:, C_ID:C_ID + P]
        mask = consts[:, C_MASK:C_MASK + 32]
        half = consts[:, C_HALF:C_HALF + GT]

        s_const = sem("s_const")
        s_x = [[sem(f"s_patches{b}{t}") for t in range(GT)] for b in range(2)]
        s_tokw = sem("s_tokw")
        s_wraw = [sem(f"s_wraw_{n}") for n in "qkv"]
        s_graw = sem("s_graw")
        s_gateb = sem("s_gateb")
        s_wo = sem("s_wo")
        s_bo = sem("s_bo")
        s_packh = sem("s_packh")
        s_packl = sem("s_packl")
        s_zero = sem("s_zero")
        s_e = sem("s_e")
        s_row = sem("s_row")
        s_res = sem("s_res")
        s_t0 = sem("s_t0")
        s_hi0 = sem("s_hi0")
        s_lo0 = sem("s_lo0")
        s_qkv = sem("s_qkv")
        s_qevac = sem("s_qevac")
        s_sc = sem("s_sc")
        s_soft = sem("s_soft")
        s_exp = sem("s_exp")
        s_pt = sem("s_pt")
        s_av = sem("s_av")
        s_ot = sem("s_ot")
        s_o = sem("s_o")
        s_ln = sem("s_ln")
        s_ve = sem("s_ve")
        s_rstd = sem("s_rstd")
        s_x1 = sem("s_x1")
        s_acc = sem("s_acc")
        s_t1 = sem("s_t1")
        s_hi1 = sem("s_hi1")
        s_lo1 = sem("s_lo1")
        s_lg = sem("s_lg")
        s_lgc = sem("s_lgc")
        s_lgt = sem("s_lgt")
        s_logit = sem("s_logit")
        s_fb2 = sem("s_fb2")
        s_lnb = sem("s_lnb")
        s_w2 = [sem(f"s_w2{k}") for k in range(2)]
        s_weigh = sem("s_weigh")
        s_cr = sem("s_cr")
        s_w1 = sem("s_w1pre")
        s_small = sem("s_small1")

        block = ctx.enter_context(nc.Block())

        @block.sync
        def _(sp):
            def load_tile(g, b, t):
                sp.dma_start(xin[b][:, t, :, :], ins["patches"][bass.ds(g * GT + t, 1), :, :, :]
                             .rearrange("o p c n -> (o p) c n")).then_inc(s_x[b][t], 16)

            def load_x(g, b):
                need(sp, s_e, g - 1)
                for t in range(GT):
                    load_tile(g, b, t)

            def load_w2(g):
                need(sp, s_cr, 2 * g)
                for k in range(2):
                    sp.dma_start(w2raw[k][:, :, :], ins["fc2_w"][bass.ds(2 * g + k, 1), :, :, :]
                                 .rearrange("o p c n -> (o p) c n")).then_inc(s_w2[k], 16)

            load_tile(0, 0, 0)
            sp.dma_start(tokw[:, :, :], ins["tok_w"]).then_inc(s_tokw, 16)
            load_tile(0, 0, 1)
            sp.dma_start(wraw[0], ins["w_qkv"][0]).then_inc(s_wraw[0], 16)
            sp.dma_start(consts[:, :], ins["consts"]).then_inc(s_const, 16)
            sp.dma_start(wraw[1], ins["w_qkv"][1]).then_inc(s_wraw[1], 16)
            sp.dma_start(wraw[2], ins["w_qkv"][2]).then_inc(s_wraw[2], 16)
            sp.dma_start(bo[:, :], ins["b_o"].to_broadcast([P, D])).then_inc(s_bo, 16)
            sp.dma_start(graw[:, :, :], ins["gate_w"]).then_inc(s_graw, 16)
            load_x(1, 1)
            sp.dma_start(lnb[:, :, :], ins["ln_b"]).then_inc(s_lnb, 16)
            load_w2(0)
            sp.dma_start(wo[:, :, :], ins["w_o"]).then_inc(s_wo, 16)
            sp.dma_start(gateb[:, :], ins["gate_b"].to_broadcast([P, E])).then_inc(s_gateb, 16)
            sp.dma_start(crep[:, :], ins["fc2_b"]).then_inc(s_fb2, 16)
            sp.dma_start(lnw[:, :, :], ins["ln_w"]).then_inc(s_small, 16)
            for k in range(2):
                sp.dma_start(fb1[k][:, :], ins["fc1_b"][k]).then_inc(s_small, 16)
            sp.wait_ge(s_packl, 1)
            sp.dma_start(wbuf[:, :].rearrange("p (e n) -> p e n", e=2),
                         ins["fc1_w"][0:2].rearrange("e p c n -> p e (c n)")).then_inc(s_w1, 16)
            with sp.Fori(1, NG // 2) as turn:
                for b in range(2):
                    load_x(turn * 2 + b, b)
                    load_w2(turn * 2 + b - 1)
            load_w2(NG - 1)
            sp.wait_ge(s_cr, E)
            for k in range(2):
                sp.dma_start(w2raw[k][:, :, :], ins["fc2_w"][k]).then_inc(s_w2[k], 16)
            for k in range(2):
                sp.wait_ge(s_w2[k], 16 * (NG + 1))
            sp.wait_ge(s_small, 16 * 3)

        @block.gpsimd
        def _(pool):
            zeroed = [kT[b][r * H:r * H + H, :, 1 - r, :] for b in range(2) for r in range(2)]
            for k, part in enumerate(zeroed + [pT[t][:, :, :] for t in range(GT)]):
                need(pool, s_zero, k)
                pool.memset(part, 0.0).then_inc(s_zero, 1)
            pool.wait_ge(s_const, 16)

            def norm_group(g):
                held(pool, s_ln, 3 * GT * (g + 1))
                pool.tensor_scalar(vareps[:, :], meanvar[:, :, 1], EPS, None, ALU.add).then_inc(s_ve, 1)
                need(pool, s_ve, g + 1)
                need(pool, s_x1, g)
                pool.tensor_tensor(rstd[:, :], vareps[:, :], half, ALU.pow).then_inc(s_rstd, 1)
                held(pool, s_x1, g + 1)
                pool.tensor_copy(acc[:, bass.ds(g * GT, GT), :], x1row[:, :, 0:D]).then_inc(s_acc, 1)

            def weigh(g):
                for k in range(2):
                    count = 4 * (2 * g + k)
                    held(pool, s_cr, 2 * g + k - 1)
                    pool.tensor_tensor(strip[k][:, :], consts[:, bass.ds(C_EYE + E - 2 * g - k, P)],
                                       consts[:, C_ONES:C_ONES + P], ALU.mult).then_inc(s_weigh, 1)
                    held(pool, s_w2[k], 16 * (g + 1))
                    w = w2raw[k]
                    pool.tensor_tensor(w[:, :, :], w[:, :, :],
                                       lnb[:, bass.ds(2 * g + k, 1), :].rearrange("p o c -> p (o c)")
                                       .unsqueeze(2).to_broadcast([P, FC, D]), ALU.mult).then_inc(s_weigh, 1)
                    for c in (1, 2):
                        need(pool, s_weigh, count + 1 + c)
                        pool.tensor_tensor(w[:, 0, :], w[:, 0, :], w[:, c, :], ALU.add).then_inc(s_weigh, 1)

            pool.wait_ge(s_lnb, 16)
            weigh(0)
            weigh(1)
            norm_group(0)
            with pool.Fori(1, NG - 1) as g:
                weigh(g + 1)
                norm_group(g)
            norm_group(NG - 1)

        @block.scalar
        def _(act):
            def copy_row(g):
                need(act, s_e, g + 1)
                need(act, s_t0, g)
                need(act, s_res, g)
                rows = p_row[:, 0:GT * D].rearrange("p (t d) -> p t d", t=GT)
                act.copy(h0row[:, :, 0:D], rows)
                act.copy(h0row[:, :, D:D + DB], rows[:, :, P:D]).then_inc(s_row, 1)

            def high0(g, b):
                need(act, s_t0, g + 1)
                act.copy(h0hi[b][:, :, :], p_row[:, :].rearrange("p (c n) -> p c n", c=2)).then_inc(s_hi0, 1)

            def high1(g):
                need(act, s_t1, g + 1)
                act.copy(XH[:, :, bass.ds(g * GTOK, GTOK)],
                         p_row[:, :].rearrange("p (c n) -> p c n", c=2)).then_inc(s_hi1, 1)

            def copy_qkv(g, b, item):
                need(act, s_qkv, ITEMS * g + item + 1)
                bank = p_qkv[item % 2]
                if item < IC // 2:
                    act.copy(qT[b][:, 2 * item:2 * item + 2, :], bank[:, :].rearrange("p (c n) -> p c n", c=2)) \
                       .then_inc(s_qevac, 1)
                elif item < IC:
                    c = 2 * (item - IC // 2)
                    for r in range(2):
                        act.copy(kT[b][r * H:r * H + H, c:c + 2, r, :],
                                 bank[r * H:r * H + H, :].rearrange("p (c n) -> p c n", c=2)) \
                           .then_inc(s_qevac, 1)
                else:
                    t, part = (item - IC) // 2, (item - IC) % 2
                    act.copy(v[b][:, t, part * F:part * F + F], bank[:, 0:F]).then_inc(s_qevac, 1)

            def exps(g, t):
                need(act, s_soft, 6 * (GT * g + t) + 3)
                act.activation(probs[:, :, :], probs[:, :, :], ACT.Exp).then_inc(s_exp, 1)

            def copy_ot(g, t):
                need(act, s_av, GT * g + t + 1)
                act.copy(oT[t][:, :, :], p_o[:, 0:INNER].rearrange("p (c n) -> p c n", c=IC)).then_inc(s_ot, 1)

            def copy_logits(g):
                need(act, s_lg, g + 1)
                need(act, s_lgt, g)
                act.copy(logitT[:, :], p_lg[0:E, 0:GTOK]).then_inc(s_lgc, 1)

            copy_row(0)
            high0(0, 0)
            act.wait_ge(s_zero, 4 + GT)
            for item in range(ITEMS):
                copy_qkv(0, 0, item)

            def body(g, b):
                nxt = not (isinstance(g, int) and g == NG - 1)
                if nxt:
                    copy_row(g + 1)
                    high0(g + 1, 1 - b)
                if nxt:
                    exps(g, 0)
                    for item in range(IC // 2 + 1):
                        copy_qkv(g + 1, 1 - b, item)
                exps(g, 1)
                copy_ot(g, 0)
                if nxt:
                    for item in range(IC // 2 + 1, IC + 2):
                        copy_qkv(g + 1, 1 - b, item)
                copy_ot(g, 1)
                if not (isinstance(g, int) and g == 0):
                    high1(g - 1)
                if nxt:
                    copy_qkv(g + 1, 1 - b, IC + 2)
                if isinstance(g, int) and g == NG - 2:
                    exps(g + 1, 0)
                if nxt:
                    copy_qkv(g + 1, 1 - b, IC + 3)
                if not (isinstance(g, int) and g == 0):
                    copy_logits(g - 1)

            pairs(act, NG, body)
            high1(NG - 1)
            copy_logits(NG - 1)

        @block.vector
        def _(dve):
            def residual(g):
                need(dve, s_row, g + 1)
                dve.tensor_tensor(acc[:, bass.ds(g * GT, GT), :], h0row[:, :, 0:D],
                                  bo[:, :].unsqueeze(1).to_broadcast([P, GT, D]), ALU.add).then_inc(s_res, 1)

            def low0(g, b):
                need(dve, s_hi0, g + 1)
                dve.tensor_tensor(h0lo[b][:, :, :], p_row[:, :].rearrange("p (c n) -> p c n", c=2),
                                  h0hi[b][:, :, :].bitcast(F32), ALU.subtract).then_inc(s_lo0, 1)

            def low1(g):
                need(dve, s_hi1, g + 1)
                cols = bass.ds(g * GTOK, GTOK)
                dve.tensor_tensor(XL[:, :, cols], p_row[:, :].rearrange("p (c n) -> p c n", c=2),
                                  XH[:, :, cols].bitcast(F32), ALU.subtract).then_inc(s_lo1, 1)

            def mask_scores(g, t):
                n = GT * g + t
                need(dve, s_sc, n + 1)
                need(dve, s_pt, n)
                dve.scalar_tensor_tensor(out=probs[:, :, :], in0=p_sc[:, :, :], scalar=SCALE,
                                         in1=mask.unsqueeze(1).to_broadcast([P, HEADS, 32]),
                                         op0=ALU.mult, op1=ALU.add).then_inc(s_soft, 1)
                need(dve, s_soft, 6 * n + 1)
                dve.tensor_reduce(smax[:, :], probs[:, :, :], AX.X, ALU.max).then_inc(s_soft, 1)

            def shift_scores(g, t):
                n = GT * g + t
                need(dve, s_soft, 6 * n + 2)
                dve.tensor_tensor(probs[:, :, :], probs[:, :, :],
                                  smax[:, :].unsqueeze(2).to_broadcast([P, HEADS, 32]), ALU.subtract) \
                   .then_inc(s_soft, 1)

            def normalise(g, t):
                n = GT * g + t
                need(dve, s_exp, n + 1)
                dve.tensor_reduce(ssum[:, :], probs[:, :, :], AX.X, ALU.add).then_inc(s_soft, 1)
                need(dve, s_soft, 6 * n + 4)
                dve.reciprocal(srec[:, :], ssum[:, :]).then_inc(s_soft, 1)
                need(dve, s_soft, 6 * n + 5)
                dve.tensor_tensor(probs[:, :, :], probs[:, :, :],
                                  srec[:, :].unsqueeze(2).to_broadcast([P, HEADS, 32]), ALU.mult) \
                   .then_inc(s_soft, 1)
                need(dve, s_soft, 6 * n + 6)
                need(dve, s_av, n - 1)
                for q in range(4):
                    rows = slice(32 * q, 32 * q + 32)
                    last = dve.transpose(pT[t][rows, :, 32 * q:32 * q + 32], probs[rows, :, :])
                last.then_inc(s_pt, 1)

            def add_residual(g, t):
                n = GT * g + t
                need(dve, s_o, n + 1)
                dve.tensor_tensor(z[t][:, :], p_o[:, 0:D],
                                  acc[:, bass.ds(g * GT + t, 1), :].rearrange("p o d -> p (o d)"), ALU.add) \
                   .then_inc(s_ln, 1)
                need(dve, s_ln, 3 * n + 1)
                dve.bn_stats(stats[:, t, :], z[t][:, :]).then_inc(s_ln, 1)
                held(dve, s_ln, 3 * n + 2)
                dve.bn_aggr(meanvar[:, t, :], stats[:, t, :]).then_inc(s_ln, 1)

            def norm_rows(g):
                need(dve, s_rstd, g + 1)
                need(dve, s_t1, g)
                need(dve, s_acc, g)
                for t in range(GT):
                    for cols, part in ((slice(0, D), z[t][:, :]), (slice(D, D + DB), z[t][:, P:D])):
                        last = dve.tensor_scalar(x1row[:, t, cols], part, meanvar[:, t, 0:1], rstd[:, t:t + 1],
                                                 ALU.subtract, ALU.mult)
                last.then_inc(s_x1, 1)

            def add_gate(g):
                need(dve, s_lgt, g + 1)
                dve.tensor_tensor(logit[:, bass.ds(g * GT, GT), :],
                                  p_lg[:, GTOK:GTOK + GT * E].rearrange("p (t e) -> p t e", t=GT),
                                  gateb[:, :].unsqueeze(1).to_broadcast([P, GT, E]), ALU.add) \
                   .then_inc(s_logit, 1)

            for j in range(3):
                w = wqkv[:, :, j * INNER:(j + 1) * INNER]
                dve.wait_ge(s_wraw[j], 16)
                pack_high(dve, w, wraw[j]).then_inc(s_packh, 1)
                if j == 1:
                    low0(0, 0)
                dve.wait_ge(s_packh, j + 1)
                pack_low(dve, w, wraw[j]).then_inc(s_packl, 1)
            dve.wait_ge(s_const, 16)
            dve.wait_ge(s_bo, 16)
            residual(0)
            dve.wait_ge(s_graw, 16)
            pack_high(dve, gate_pack, graw).then_inc(s_packh, 1)
            dve.wait_ge(s_packh, 4)
            pack_low(dve, gate_pack, graw).then_inc(s_packl, 1)
            dve.wait_ge(s_gateb, 16)
            dve.wait_ge(s_zero, 4 + GT)

            def body(g, b):
                nxt = not (isinstance(g, int) and g == NG - 1)
                if nxt:
                    mask_scores(g, 0)
                    low0(g + 1, 1 - b)
                    shift_scores(g, 0)
                    normalise(g, 0)
                mask_scores(g, 1)
                shift_scores(g, 1)
                if nxt:
                    residual(g + 1)
                if not (isinstance(g, int) and g <= 1):
                    add_gate(g - 2)
                normalise(g, 1)
                add_residual(g, 0)
                if isinstance(g, int) and g == NG - 2:
                    dve.wait_ge(s_w1, 16)
                    w1raw0 = wbuf[:, 0:2 * F].rearrange("p (c n) -> p c n", c=2)
                    pack_high(dve, w1p0, w1raw0).then_inc(s_packh, 1)
                    dve.wait_ge(s_packh, 5)
                    pack_low(dve, w1p0, w1raw0).then_inc(s_packl, 1)
                if not (isinstance(g, int) and g == 0):
                    low1(g - 1)
                if isinstance(g, int) and g == NG - 2:
                    mask_scores(g + 1, 0)
                    shift_scores(g + 1, 0)
                add_residual(g, 1)
                if isinstance(g, int) and g == NG - 2:
                    normalise(g + 1, 0)
                norm_rows(g)

            pairs(dve, NG, body)
            add_gate(NG - 2)
            dve.wait_ge(s_fb2, 16)
            dve.wait_ge(s_cr, E)
            dve.tensor_tensor(crep[:, :], p_cr[:, 0:D], crep[:, :], ALU.add)
            low1(NG - 1)
            add_gate(NG - 1)

        @block.tensor
        def _(pe):
            def embed(g, b):
                need(pe, s_hi0, g)
                need(pe, s_lo0, g)
                if not isinstance(g, int) or g >= 3:
                    pe.wait_ge(s_hi1, g - 2)
                    pe.wait_ge(s_lo1, g - 2)
                for t in range(GT):
                    need(pe, s_x[b][t], 16 * ((g - b) // 2 + 1))
                    for c in range(KC):
                        mm = pe.matmul(p_row[:, t * D:t * D + D], xin[b][:, t, c, :], tokw[:, c, :],
                                       start=(c == 0), stop=(c == KC - 1))
                mm.then_inc(s_e, 1)

            def turn_rows(rows):
                for c in range(2):
                    for t in range(GT):
                        mm = pe.transpose(p_row[:, (c * GT + t) * P:(c * GT + t + 1) * P],
                                          rows[:, t, c * P:(c + 1) * P], ident)
                return mm

            def transpose0(g):
                need(pe, s_row, g + 1)
                turn_rows(h0row).then_inc(s_t0, 1)

            def transpose1(g):
                need(pe, s_x1, g + 1)
                after = min(g + 3, NG) if isinstance(g, int) else g + 3
                need(pe, s_hi0, after)
                need(pe, s_lo0, after)
                need(pe, s_hi1, g)
                need(pe, s_lo1, g)
                turn_rows(x1row).then_inc(s_t1, 1)

            def qkv(g, b, item):
                if item == 0:
                    need(pe, s_hi0, g + 1)
                    need(pe, s_lo0, g + 1)
                done = [1, 2, 3, 5, 7, 9, 10, 11, 12, 13][(item - 2) % ITEMS]
                need(pe, s_qevac, EVACS * (g if item >= 2 else g - 1) + done)
                bank = p_qkv[item % 2]
                xh, xl = h0hi[b], h0lo[b]
                if item < IC:
                    for j in range(2):
                        c = 2 * item + j
                        terms = stack_terms(wqkv[:, :, c * P:(c + 1) * P], xh, xl)
                        for k, (w, x) in enumerate(terms):
                            mm = pe.matmul(bank[:, j * GTOK:(j + 1) * GTOK], w, x,
                                           start=(k == 0), stop=(k == len(terms) - 1))
                else:
                    t, part = (item - IC) // 2, (item - IC) % 2
                    col = 2 * INNER + part * F
                    cols = slice(t * P, t * P + P)
                    terms = stack_terms(wqkv[:, :, col:col + F], xh[:, :, cols], xl[:, :, cols])
                    for k, (w, x) in enumerate(terms):
                        mm = pe.matmul(bank[:, 0:F], x, w, start=(k == 0), stop=(k == len(terms) - 1))
                mm.then_inc(s_qkv, 1)

            def score(g, b, t):
                need(pe, s_qevac, EVACS * g + 3 * (IC // 2))
                need(pe, s_soft, 6 * (GT * g + t - 1) + 1)
                for c in range(IC):
                    for q in range(4):
                        cols = slice(t * P + 32 * q, t * P + 32 * q + 32)
                        mm = pe.matmul(p_sc[32 * q:32 * q + 32, 2 * c:2 * c + 2, :], qT[b][:, c, cols],
                                       kT[b][:, c, :, cols], start=True, stop=True)
                mm.then_inc(s_sc, 1)

            def attend(g, b, t):
                n = GT * g + t
                need(pe, s_qevac, EVACS * (g + 1))
                need(pe, s_pt, n + 1)
                need(pe, s_ln, 3 * (n - 1) + 1)
                for h in range(HEADS):
                    r = (h % 2) * H
                    mm = pe.matmul(p_o[r:r + H, (h // 2) * P:(h // 2 + 1) * P], v[b][:, t, h * DH:(h + 1) * DH],
                                   pT[t][:, h, :], start=True, stop=True)
                mm.then_inc(s_av, 1)

            def project(g, t):
                need(pe, s_ot, GT * g + t + 1)
                for c in range(IC):
                    mm = pe.matmul(p_o[:, 0:D], oT[t][:, c, :], wo[:, c, :], start=(c == 0), stop=(c == IC - 1))
                mm.then_inc(s_o, 1)

            def router(g):
                need(pe, s_hi1, g + 1)
                need(pe, s_lo1, g + 1)
                need(pe, s_logit, g)
                cols = bass.ds(g * GTOK, GTOK)
                terms = stack_terms(gate_pack, XH[:, :, cols], XL[:, :, cols])
                for k, (w, x) in enumerate(terms):
                    mm = pe.matmul(p_lg[0:E, 0:GTOK], w, x, start=(k == 0), stop=(k == len(terms) - 1))
                mm.then_inc(s_lg, 1)

            def turn_logits(g):
                held(pe, s_lgc, g + 1)
                for t in range(GT):
                    mm = pe.transpose(p_lg[:, GTOK + t * E:GTOK + (t + 1) * E], logitT[:, t * P:(t + 1) * P],
                                      ident[0:E, 0:E])
                mm.then_inc(s_lgt, 1)

            def constant_rows(g, k):
                need(pe, s_weigh, 4 * (2 * g + k + 1))
                first, last = (isinstance(g, int) and g == n and k == m for n, m in ((0, 0), (NG - 1, 1)))
                mm = pe.matmul(p_cr[:, 0:D], strip[k][:, :], w2raw[k][:, 0, :], start=first, stop=last,
                               skip_group_check=True)
                mm.then_inc(s_cr, 1)

            def first_hidden(f):
                pe.wait_ge(s_qevac, EVACS * NG)
                if f == 2:
                    pe.wait_ge(s_soft, 6 * (NT - 1) + 1)
                pe.wait_ge(s_hi1, ST // GT)
                pe.wait_ge(s_lo1, ST // GT)
                pe.wait_ge(s_packl, 5)
                hidden_chunk(pe, p_h[f], w1p0, XH, XL, f, 0).then_inc(s_g1, 1)

            pe.wait_ge(s_tokw, 16)
            embed(0, 0)
            pe.wait_ge(s_const, 16)
            transpose0(0)
            for item in range(ITEMS):
                pe.wait_ge(s_packl, min(3, 1 + item // (IC // 2)))
                qkv(0, 0, item)
            pe.wait_ge(s_zero, 4 + GT)
            pe.wait_ge(s_wo, 16)

            def body(g, b):
                nxt = not (isinstance(g, int) and g == NG - 1)
                if nxt:
                    embed(g + 1, 1 - b)
                if not (isinstance(g, int) and g <= 1):
                    turn_logits(g - 2)
                if nxt:
                    score(g, b, 0)
                    transpose0(g + 1)
                constant_rows(g, 0)
                score(g, b, 1)
                constant_rows(g, 1)
                if not nxt:
                    first_hidden(0)
                    first_hidden(1)
                if nxt:
                    for item in range(IC // 2 + 1):
                        qkv(g + 1, 1 - b, item)
                attend(g, b, 0)
                if not nxt:
                    first_hidden(2)
                if nxt:
                    for item in range(IC // 2 + 1, IC):
                        qkv(g + 1, 1 - b, item)
                project(g, 0)
                if nxt:
                    for item in range(IC, IC + 2):
                        qkv(g + 1, 1 - b, item)
                attend(g, b, 1)
                if not (isinstance(g, int) and g == 0):
                    transpose1(g - 1)
                if nxt:
                    qkv(g + 1, 1 - b, IC + 2)
                if isinstance(g, int) and g == NG - 2:
                    score(g + 1, 1 - b, 0)
                project(g, 1)
                if nxt:
                    qkv(g + 1, 1 - b, IC + 3)
                if not (isinstance(g, int) and g == 0):
                    router(g - 1)

            pairs(pe, NG, body)
            turn_logits(NG - 2)
            transpose1(NG - 1)
            router(NG - 1)
            turn_logits(NG - 1)


def experts(nc, ins, consts, XH, XL, acc, logit, crep, lnw, fb1, wbuf, w1p0, w2raw, p_h, s_g1, out):
    with ExitStack() as ctx:
        def sb(name, shape, dt=F32):
            return ctx.enter_context(nc.sbuf_tensor(name, shape, dt))

        def ps(name, shape):
            return ctx.enter_context(nc.psum_tensor(name, shape, F32))

        def sem(name):
            return ctx.enter_context(nc.semaphore(name))

        w1raw = [wbuf[:, b * 2 * F:(b + 1) * 2 * F].rearrange("p (c n) -> p c n", c=2) for b in range(2)]
        w1p = [w1p0, sb("w1p1", [P, 4, F], F32R)]
        w2s = sb("w2s", [P, FC, D])
        w2t = sb("w2t", [P, D])
        w2c = sb("w2c", [P, FC, D])
        c_hi = [sb(f"c_hi{b}", [P, FC, CW], F32R) for b in range(2)]
        c_lo = [sb(f"c_lo{b}", [P, FC, CW], F32R) for b in range(2)]
        g = [sb(f"g{b}", [P, FC, STOK]) for b in range(2)]
        g_hi = [sb(f"g_hi{b}", [P, FC, STOK], F32R) for b in range(2)]
        g_lo = [sb(f"g_lo{b}", [P, FC, STOK], F32R) for b in range(2)]
        sq = sb("sq", [P, FC, STOK])
        sq01 = sb("sq01", [P, STOK])
        sqsum = [sb(f"sqsum{b}", [P, STOK]) for b in range(2)]
        sqT = sb("sqT", [P, STOK])
        sqq = sb("sqq", [P, STOK // 32])
        sqp = [sb(f"sqp{b}", [P, STOK // 32, 2], F32R) for b in range(2)]
        fold = sb("fold", [P, P], F32R)
        sums = [sb(f"sums{b}", [P, ST]) for b in range(2)]
        sqm = sb("sqm", [P, ST, 8])
        sqn = [sb(f"sqn{b}", [P, ST]) for b in range(2)]
        sumg2 = sb("sumg2", [P, ST])
        varn = sb("varn", [P, ST])
        vare = sb("vare", [P, ST])
        rn = sb("rn", [P, ST])
        scale = [sb(f"scale{b}", [P, ST]) for b in range(2)]
        lmax = sb("lmax", [P, NT])
        lsum = sb("lsum", [P, NT])
        lrec = sb("lrec", [P, NT])
        prob = sb("prob", [P, NT, E + 8])
        top8 = sb("top8", [P, NT, 8])
        marked = sb("marked", [P, NT, E + 8])
        comb = sb("comb", [P, NT, E])
        combn = sb("combn", [P, E, NT])
        combT = sb("combT", [P, 2, P])
        crows = sb("crows", [P, 8, D])
        st2 = sb("st2", [P, NT, 6])
        mv2 = sb("mv2", [P, NT, 2])
        ve2 = sb("ve2", [P, NT])
        rs2 = sb("rs2", [P, NT])
        shift2 = sb("shift2", [P, NT])
        res = sb("res", [P, NT, D])

        p_w = ps("p_w", [P, 512])
        p_y = [ps(f"p_y{b}", [P, ST, YW]) for b in range(2)]

        ident = consts[:, C_ID:C_ID + P]
        ones = consts[:, C_ONES:C_ONES + P]
        rowmask = consts[:, C_ROW:C_ROW + 8]
        half = consts[:, C_HALF:C_HALF + NT]
        quad = consts[:, C_QUAD:C_QUAD + 8]

        s_w1 = [sem(f"s_w1raw{b}") for b in range(2)]
        s_b1 = [sem(f"s_b1{b}") for b in range(2)]
        s_w2 = [sem(f"s_w2raw{b}") for b in range(2)]
        s_ph = sem("s_ph")
        s_w1p = sem("s_w1p")
        s_w2s = sem("s_w2s")
        s_mean = sem("s_mean")
        s_cen = sem("s_cen")
        s_chi = sem("s_chi")
        s_cp = sem("s_cp")
        s_pad = sem("s_pad")
        s_r = sem("s_r")
        s_rexp = sem("s_rexp")
        s_crow = sem("s_crow")
        s_combt = sem("s_combt")
        s_combs = sem("s_combs")
        s_init = sem("s_init")
        s_initd = sem("s_initd")
        s_gelu = sem("s_gelu")
        s_sq = sem("s_sq")
        s_sq01 = sem("s_sq01")
        s_sqs = sem("s_sqs")
        s_sqt = sem("s_sqt")
        s_sqq = sem("s_sqq")
        s_hi = sem("s_hi")
        s_lo = sem("s_lo")
        s_y = sem("s_y")
        s_sums = sem("s_sums")
        s_v = sem("s_v")
        s_scale = sem("s_scale")
        s_ev = sem("s_ev")
        s_f = sem("s_f")
        s_fa = sem("s_fa")
        s_fp = sem("s_fp")
        s_shift = sem("s_shift")
        s_res = sem("s_res2")
        s_resv = sem("s_resv")
        s_out = sem("s_out")

        block = ctx.enter_context(nc.Block())

        @block.sync
        def _(sp):
            def load_bias(e, b):
                need(sp, s_gelu, FC * NQ * (e - 1))
                sp.dma_start(fb1[b][:, :], ins["fc1_b"][bass.ds(e, 1), :, :].rearrange("o p c -> (o p) c")) \
                   .then_inc(s_b1[b], 16)

            def load_weights(e, b):
                need(sp, s_w1p, e - 1)
                sp.dma_start(w1raw[b], ins["fc1_w"][bass.ds(e, 1), :, :, :]
                             .rearrange("o p c n -> (o p) c n")).then_inc(s_w1[b], 16)
                need(sp, s_w2s, 3 * (e - 2) + 1)
                sp.dma_start(w2raw[b][:, :, :], ins["fc2_w"][bass.ds(e, 1), :, :, :]
                             .rearrange("o p c n -> (o p) c n")).then_inc(s_w2[b], 16)
                load_bias(e, b)

            with sp.Fori(1, E // 2) as turn:
                for b in range(2):
                    load_weights(turn * 2 + b, b)
            for t in range(NT):
                if t < NT - 2:
                    sp.wait_ge(s_res, t + 1)
                else:
                    sp.wait_ge(s_resv, t - (NT - 3))
                sp.dma_start(out[t * P:(t + 1) * P, :], res[:, t, :]).then_inc(s_out, 16)
            sp.wait_ge(s_out, 16 * NT)

        @block.gpsimd
        def _(pool):
            def scale_w2(e, b):
                need(pool, s_w2[b], 16 * ((e - b) // 2))
                need(pool, s_cen, e)
                pool.tensor_tensor(w2s[:, :, :], w2raw[b][:, :, :],
                                   lnw[:, bass.ds(e, 1), :].rearrange("p o c -> p (o c)")
                                   .unsqueeze(2).to_broadcast([P, FC, D]), ALU.mult).then_inc(s_w2s, 1)
                need(pool, s_w2s, 3 * e + 1)
                pool.tensor_tensor(w2t[:, :], w2s[:, 0, :], w2s[:, 1, :], ALU.add).then_inc(s_w2s, 1)
                need(pool, s_w2s, 3 * e + 2)
                pool.tensor_tensor(w2t[:, :], w2t[:, :], w2s[:, 2, :], ALU.add).then_inc(s_w2s, 1)

            def sum_squares(i, b):
                need(pool, s_sq, i + 1)
                need(pool, s_sqs, i)
                pool.tensor_tensor(sq01[:, :], sq[:, 0, :], sq[:, 1, :], ALU.add).then_inc(s_sq01, 1)
                need(pool, s_sq01, i + 1)
                need(pool, s_sqt, i - 1)
                pool.tensor_tensor(sqsum[b][:, :], sq01[:, :], sq[:, 2, :], ALU.add).then_inc(s_sqs, 1)

            def factors(i, b, expert, q):
                need(pool, s_sums, 3 * i + 3)
                pool.tensor_tensor(sumg2[:, :], sums[b][:, :], sums[b][:, :], ALU.mult).then_inc(s_v, 1)
                need(pool, s_v, 4 * i + 1)
                pool.tensor_tensor(varn[:, :], sqn[b][:, :], sumg2[:, :], ALU.subtract).then_inc(s_v, 1)
                held(pool, s_v, 4 * i + 2)
                pool.tensor_scalar(vare[:, :], varn[:, :], 0.0, EPS * F * F, ALU.max, ALU.add).then_inc(s_v, 1)
                need(pool, s_v, 4 * i + 3)
                pool.tensor_tensor(rn[:, :], vare[:, :], half[:, 0:ST], ALU.pow).then_inc(s_v, 1)
                need(pool, s_v, 4 * i + 4)
                need(pool, s_ev, i - 1)
                pool.tensor_tensor(scale[b][:, :], rn[:, :],
                                   combn[:, bass.ds(expert, 1), q * ST:(q + 1) * ST].rearrange("p o t -> p (o t)"),
                                   ALU.mult).then_inc(s_scale, 1)

            def final_deviation(q):
                tiles = slice(q * ST, (q + 1) * ST)
                pool.wait_ge(s_fa, (q + 1) * ST)
                pool.tensor_scalar(ve2[:, tiles], mv2[:, tiles, 1], EPS, None, ALU.add).then_inc(s_fp, 1)
                pool.wait_ge(s_fp, 2 * q + 1)
                pool.tensor_tensor(rs2[:, tiles], ve2[:, tiles], half[:, 0:ST], ALU.pow).then_inc(s_fp, 1)

            scale_w2(0, 0)
            for b in range(2):
                pool.memset(c_hi[b][:, :, D:D + 1].bitcast(F32), 1.0)
                pool.memset(c_hi[b][:, :, D + 1:CW].bitcast(F32), 0.0)
                last = pool.memset(c_lo[b][:, :, D:CW].bitcast(F32), 0.0)
            last.then_inc(s_pad, 1)
            pool.tensor_tensor(crows[:, :, :], crep[:, :].unsqueeze(1).to_broadcast([P, 8, D]),
                               rowmask.unsqueeze(2).to_broadcast([P, 8, D]), ALU.mult).then_inc(s_crow, 1)

            def body(e, b):
                last = isinstance(e, int) and e == E - 1
                for q in range(NQ):
                    i = e * NQ + q
                    sum_squares(i, q % 2)
                    if isinstance(e, int) and i == 1:
                        pool.wait_ge(s_r, R_COMBN)
                    if not (isinstance(e, int) and i == 0):
                        factors(i - 1, (q + 1) % 2, e if q else e - 1, (q - 1) % NQ)
                    if q == 0 and not last:
                        scale_w2(e + 1, 1 - b)
                    if last and q >= 2:
                        final_deviation(q - 2)

            pairs(pool, E, body)
            factors(STEPS - 1, (NQ - 1) % 2, E - 1, NQ - 1)
            for q in (NQ - 2, NQ - 1):
                final_deviation(q)

        @block.scalar
        def _(act):
            def gelus(i, b, e_b):
                for f in range(FC):
                    need(act, s_g1, FC * i + f + 1)
                    need(act, s_lo, FC * (i - 2) + f + 1)
                    if f == 0:
                        need(act, s_sq, i - 1)
                    act.activation(g[b][:, f, :], p_h[f][:, :], ACT.Gelu, bias=fb1[e_b][:, f:f + 1]) \
                       .then_inc(s_gelu, 1)
                    need(act, s_gelu, FC * i + f + 1)
                    if f == 0:
                        need(act, s_y, i - 1)
                    act.copy(g_hi[b][:, f, :], g[b][:, f, :]).then_inc(s_hi, 1)
                need(act, s_sqs, i)
                act.activation(sq[:, :, :], g[b][:, :, :], ACT.Square).then_inc(s_sq, 1)

            act.wait_ge(s_r, 3)
            act.activation(prob[:, :, 0:E], logit[:, :, :], ACT.Exp).then_inc(s_rexp, 1)

            def body(e, b):
                need(act, s_b1[b], 16 * ((e - b) // 2))
                for q in range(NQ):
                    gelus(e * NQ + q, q % 2, b)

            pairs(act, E, body)
            for t in range(NT - 2):
                act.wait_ge(s_shift, t // ST + 1)
                act.activation(res[:, t, :], acc[:, t, :], ACT.Identity, bias=shift2[:, t:t + 1],
                               scale=rs2[:, t:t + 1]).then_inc(s_res, 1)

        @block.vector
        def _(dve):
            def pack_w1(e, b):
                need(dve, s_w1[b], 16 * ((e - b) // 2))
                need(dve, s_g1, FC * NQ * (e - 1))
                pack_high(dve, w1p[b], w1raw[b]).then_inc(s_ph, 1)
                need(dve, s_ph, e)
                pack_low(dve, w1p[b], w1raw[b]).then_inc(s_w1p, 1)

            def pack_w2(e, b):
                need(dve, s_mean, e + 1)
                dve.scalar_tensor_tensor(out=w2c[:, :, :], in0=p_w[:, 0:D].unsqueeze(1).to_broadcast([P, FC, D]),
                                         scalar=-1.0 / F, in1=w2s[:, :, :], op0=ALU.mult, op1=ALU.add) \
                   .then_inc(s_cen, 1)
                need(dve, s_cen, e + 1)
                need(dve, s_y, NQ * (e - 1))
                dve.tensor_copy(c_hi[b][:, :, 0:D], w2c[:, :, :]).then_inc(s_chi, 1)
                need(dve, s_chi, e + 1)
                dve.tensor_tensor(c_lo[b][:, :, 0:D], w2c[:, :, :], c_hi[b][:, :, 0:D].bitcast(F32),
                                  ALU.subtract).then_inc(s_cp, 1)

            def split(i, b, f):
                need(dve, s_hi, FC * i + f + 1)
                if f == 0:
                    need(dve, s_y, i - 1)
                dve.tensor_tensor(g_lo[b][:, f, :], g[b][:, f, :], g_hi[b][:, f, :].bitcast(F32),
                                  ALU.subtract).then_inc(s_lo, 1)

            def fold_squares(i, b):
                need(dve, s_sqs, i + 1)
                need(dve, s_sqq, 3 * i)
                need(dve, s_y, i - 1)
                dve.transpose(sqT[:, :], sqsum[b][:, :]).then_inc(s_sqt, 1)
                need(dve, s_sqt, i + 1)
                dve.tensor_reduce(sqq[:, :], sqT[:, :].rearrange("p (n k) -> p n k", k=32), AX.X, ALU.add) \
                   .then_inc(s_sqq, 1)
                need(dve, s_sqq, 3 * i + 1)
                dve.tensor_copy(sqp[b][:, :, 0], sqq[:, :]).then_inc(s_sqq, 1)
                need(dve, s_sqq, 3 * i + 2)
                dve.tensor_tensor(sqp[b][:, :, 1], sqq[:, :], sqp[b][:, :, 0].bitcast(F32), ALU.subtract) \
                   .then_inc(s_sqq, 1)

            def copy_sums(i, b):
                need(dve, s_y, i + 1)
                need(dve, s_v, 4 * (i - 2) + 2)
                dve.tensor_copy(sums[b][:, :], p_y[b][:, :, SUMG]).then_inc(s_sums, 1)
                need(dve, s_sums, 3 * (i - 1) + 3)
                dve.tensor_tensor(sqm[:, :, :], p_y[b][:, 0, SUMSQ:SUMSQ + STOK // 16]
                                  .rearrange("p (t k) -> p t k", k=8),
                                  quad.unsqueeze(1).to_broadcast([P, ST, 8]), ALU.mult).then_inc(s_sums, 1)
                need(dve, s_sums, 3 * i + 2)
                dve.tensor_reduce(sqn[b][:, :], sqm[:, :, :], AX.X, ALU.add).then_inc(s_sums, 1)

            def add_out(i, b, q):
                need(dve, s_scale, i + 1)
                need(dve, s_ev, i - NQ + 1)
                for t in range(ST):
                    tile = acc[:, q * ST + t, :]
                    last = dve.scalar_tensor_tensor(out=tile, in0=p_y[b][:, t, 0:D], scalar=scale[b][:, t:t + 1],
                                                    in1=tile, op0=ALU.mult, op1=ALU.add)
                last.then_inc(s_ev, 1)

            step = [0]

            def r(ins):
                step[0] += 1
                ins.then_inc(s_r, 1)
                dve.wait_ge(s_r, step[0])

            def router_logits():
                dve.tensor_copy(fold[:, :], consts[:, C_FOLD:C_FOLD + P])
                dve.memset(prob[:, :, E:E + 8], -1.0)
                r(dve.memset(logit[:, :, 0:SHARED], NEG_INF))
                r(dve.tensor_reduce(lmax[:, :], logit[:, :, :], AX.X, ALU.max))
                r(dve.tensor_tensor(logit[:, :, :], logit[:, :, :],
                                    lmax[:, :].unsqueeze(2).to_broadcast([P, NT, E]), ALU.subtract))

            def router_probs():
                dve.wait_ge(s_rexp, 1)
                r(dve.tensor_reduce(lsum[:, :], prob[:, :, 0:E], AX.X, ALU.add))
                r(dve.reciprocal(lrec[:, :], lsum[:, :]))
                r(dve.tensor_tensor(prob[:, :, 0:E], prob[:, :, 0:E],
                                    lrec[:, :].unsqueeze(2).to_broadcast([P, NT, E]), ALU.mult))
                for t in range(NT):
                    last = dve.max(top8[:, t, :], prob[:, t, :])
                r(last)

            def router_weights():
                r(dve.memset(top8[:, :, ROUTE:8], -1.0))
                for t in range(NT):
                    last = dve.match_replace(marked[:, t, :], top8[:, t, :], prob[:, t, :], -2.0)
                r(last)
                r(dve.scalar_tensor_tensor(out=comb[:, :, :], in0=marked[:, :, 0:E], scalar=-2.0,
                                           in1=prob[:, :, 0:E], op0=ALU.is_equal, op1=ALU.mult))
                r(dve.tensor_scalar(comb[:, :, 0:SHARED], comb[:, :, 0:SHARED], 1.0, None, ALU.add))
                r(dve.tensor_scalar(combn[:, :, :].rearrange("p e t -> p t e"), comb[:, :, :], float(F), None,
                                    ALU.mult))
                assert step[0] == R_COMBN

            def copy_comb():
                dve.wait_ge(s_combt, 1)
                dve.tensor_copy(combT[:, :, :], p_w[:, 0:2 * P].rearrange("p (c n) -> p c n", c=2)) \
                   .then_inc(s_combs, 1)

            def add_constant(j):
                dve.wait_ge(s_init, j + 1)
                dve.tensor_tensor(acc[:, 2 * j:2 * j + 2, :], p_w[:, 0:2 * D].rearrange("p (t d) -> p t d", t=2),
                                  acc[:, 2 * j:2 * j + 2, :], ALU.add).then_inc(s_initd, 1)

            def final_stats(q):
                dve.wait_ge(s_ev, STEPS - NQ + q + 1)
                for t in range(q * ST, (q + 1) * ST):
                    dve.bn_stats(st2[:, t, :], acc[:, t, :]).then_inc(s_f, 1)
                for t in range(q * ST, (q + 1) * ST):
                    dve.wait_ge(s_f, 1 + t)
                    dve.bn_aggr(mv2[:, t, :], st2[:, t, :]).then_inc(s_fa, 1)

            def final_shift(q):
                tiles = slice(q * ST, (q + 1) * ST)
                dve.wait_ge(s_fp, 2 * q + 2)
                dve.scalar_tensor_tensor(out=shift2[:, tiles], in0=mv2[:, tiles, 0], scalar=-1.0, in1=rs2[:, tiles],
                                         op0=ALU.mult, op1=ALU.mult).then_inc(s_shift, 1)

            router_logits()
            router_probs()
            dve.wait_ge(s_pad, 1)
            pack_w2(0, 0)
            for f in range(FC):
                split(0, 0, f)

            def body(e, b):
                last = isinstance(e, int) and e == E - 1
                first = isinstance(e, int) and e == 0
                for q in range(NQ):
                    i = e * NQ + q
                    constants = isinstance(e, int) and (e, q) in CONSTANT_AT
                    more = not (last and q == NQ - 1)
                    if not (first and q == 0):
                        copy_sums(i - 1, (q + 1) % 2)
                    if constants:
                        add_constant(2 * CONSTANT_AT.index((e, q)))
                    if first and q == 0:
                        pack_w1(1, 1)
                    if more:
                        split(i + 1, (q + 1) % 2, 0)
                    fold_squares(i, q % 2)
                    if more:
                        split(i + 1, (q + 1) % 2, 1)
                        split(i + 1, (q + 1) % 2, 2)
                    if constants:
                        add_constant(2 * CONSTANT_AT.index((e, q)) + 1)
                    if first and q == 0:
                        router_weights()
                    else:
                        if last and q == NQ - 1:
                            final_stats(1)
                            final_shift(0)
                        else:
                            add_out(i - 1, (q + 1) % 2, (q - 1) % NQ)
                    if q == 0 and not first and not last:
                        pack_w1(e + 1, 1 - b)
                    if first and q == 2:
                        copy_comb()
                    if q == (1 if isinstance(e, int) and e <= 1 else 2) and not last:
                        pack_w2(e + 1, 1 - b)
                    if last and q == 1:
                        final_stats(0)

            pairs(dve, E, body)
            copy_sums(STEPS - 1, (NQ - 1) % 2)
            add_out(STEPS - 2, NQ % 2, NQ - 2)
            final_stats(NQ - 2)
            final_shift(NQ - 3)
            add_out(STEPS - 1, (NQ - 1) % 2, NQ - 1)
            final_shift(NQ - 2)
            final_stats(NQ - 1)
            final_shift(NQ - 1)
            for t in (NT - 2, NT - 1):
                dve.tensor_scalar(res[:, t, :], acc[:, t, :], mv2[:, t, 0:1], rs2[:, t:t + 1],
                                  ALU.subtract, ALU.mult).then_inc(s_resv, 1)

        @block.tensor
        def _(pe):
            def hidden(i, b, q, chunks=range(FC)):
                for f in chunks:
                    need(pe, s_gelu, FC * (i - 1) + f + 1)
                    hidden_chunk(pe, p_h[f], w1p[b], XH, XL, f, q).then_inc(s_g1, 1)

            def outputs(i, b, par):
                need(pe, s_lo, FC * (i + 1))
                need(pe, s_ev, i - 1)
                for t in (2, 3, 0, 1):
                    cols = slice(t * P, t * P + P)
                    for f in range(FC):
                        for k, (gx, wx) in enumerate(((g_hi, c_hi), (g_hi, c_lo), (g_lo, c_hi))):
                            pe.matmul(p_y[par][:, t, 0:CW], gx[par][:, f, cols], wx[b][:, f, :],
                                      start=(t % 2 == 0 and f == 0 and k == 0), stop=(f == FC - 1 and k == 2),
                                      skip_group_check=True)
                need(pe, s_sqq, 3 * (i + 1))
                pe.matmul(p_y[par][:, 0, SUMSQ:SUMSQ + STOK // 16], fold[:, :], sqp[par][:, :, :],
                          start=False, stop=True, skip_group_check=True).then_inc(s_y, 1)

            def column_sums(e):
                need(pe, s_w2s, 3 * (e + 1))
                need(pe, s_cen, e)
                if not (isinstance(e, int) and e <= 1):
                    pe.wait_ge(s_initd, NT // 4 if isinstance(e, int) and e == 2 else NT // 2)
                pe.matmul(p_w[:, 0:D], ones, w2t[:, :], start=True, stop=True).then_inc(s_mean, 1)

            def turn_comb():
                pe.wait_ge(s_r, R_COMBN)
                pe.wait_ge(s_cen, 2)
                for j in range(2):
                    mm = pe.transpose(p_w[:, j * P:(j + 1) * P],
                                      comb[:, 8 * j:8 * j + 8, :].rearrange("p t e -> p (t e)"), ident)
                mm.then_inc(s_combt, 1)

            def constant(j):
                pe.wait_ge(s_crow, 1)
                pe.wait_ge(s_combs, 1)
                need(pe, s_initd, j)
                pe.wait_ge(s_cen, 3 if j >= NT // 4 else 2)
                for t in (2 * j, 2 * j + 1):
                    mm = pe.matmul(p_w[:, (t % 2) * D:(t % 2 + 1) * D], combT[:, t // 8, :], crows[:, t % 8, :],
                                   start=True, stop=True)
                mm.then_inc(s_init, 1)

            column_sums(0)

            def body(e, b):
                last = isinstance(e, int) and e == E - 1
                for q in range(NQ):
                    i = e * NQ + q
                    if q < NQ - 1:
                        following = (i + 1, b, q + 1)
                    elif not last:
                        need(pe, s_w1p, e + 1)
                        following = (i + 1, 1 - b, 0)
                    else:
                        following = None
                    if isinstance(e, int) and (e, q) in CONSTANT_AT:
                        hidden(*following, [0])
                        constant(2 * CONSTANT_AT.index((e, q)))
                        hidden(*following, [1, 2])
                        constant(2 * CONSTANT_AT.index((e, q)) + 1)
                    elif following:
                        hidden(*following)
                    if q == 1 and not last:
                        column_sums(e + 1)
                    if q == 0:
                        need(pe, s_cp, e + 1)
                    outputs(i, b, q % 2)
                    if isinstance(e, int) and (e, q) == (0, 2):
                        turn_comb()

            pairs(pe, E, body)


R_COMBN = 12
CONSTANT_AT = [(0, 3), (1, 0), (1, 2), (1, 3)]


def vit_layer(nc, ins, out):
    with ExitStack() as ctx:
        def sb(name, shape, dt=F32):
            return ctx.enter_context(nc.sbuf_tensor(name, shape, dt))

        consts = sb("consts", [P, C_END])
        gate_pack = sb("gate_pack", [P, 4, E], F32R)
        XH = sb("XH", [P, 2, TOK], F32R)
        XL = sb("XL", [P, 2, TOK], F32R)
        acc = sb("acc", [P, NT, D])
        logit = sb("logit", [P, NT, E])
        crep = sb("crep", [P, D])
        lnb = sb("lnb", [P, E, FC])
        lnw = sb("lnw", [P, E, FC])
        fb1 = [sb(f"fb1{b}", [P, FC]) for b in range(2)]
        wbuf = sb("wbuf", [P, 4 * F])
        w1p0 = sb("w1p0", [P, 4, F], F32R)
        w2raw = [sb(f"w2raw{k}", [P, FC, D]) for k in range(2)]
        p_h = [ctx.enter_context(nc.psum_tensor(f"p_h{f}", [P, STOK], F32)) for f in range(FC)]
        s_g1 = ctx.enter_context(nc.semaphore("s_g1"))
        attention(nc, ins, consts, gate_pack, XH, XL, acc, logit, crep, lnb, lnw, fb1, wbuf, w1p0, w2raw, p_h, s_g1)
        experts(nc, ins, consts, XH, XL, acc, logit, crep, lnw, fb1, wbuf, w1p0, w2raw, p_h, s_g1, out)


def kernel(**inputs):
    import numpy as np
    import concourse.bacc as bacc
    from concourse.bass_utils import run_bass_kernel_spmd

    a = {k: np.asarray(x) for k, x in inputs.items()}

    def doubled(w):
        return np.stack([w[:P], np.concatenate([w[P:], w[P:]])], axis=1)

    def by_chunk(w, c):
        return w.reshape(c, P, -1).transpose(1, 0, 2)

    x = a["x"].reshape(IMAGES, CHANNELS, SIDE // PATCH, PATCH, SIDE // PATCH, PATCH)
    x = x.transpose(3, 5, 1, 0, 2, 4).reshape(KC, P, NT, P).transpose(2, 1, 0, 3)
    consts = np.zeros((P, C_END), np.float32)
    consts[:, C_ID:C_ID + P] = np.eye(P)
    rows = np.arange(P)
    other = (rows[:, None] % 32) // SEQ != np.arange(32)[None, :] // SEQ
    consts[:, C_MASK:C_MASK + 32][other] = MASKED
    consts[:, C_ONES:C_ONES + P] = 1.0
    consts[:, C_ROW:C_ROW + 8] = rows[:, None] // E == np.arange(8)[None, :]
    consts[:, C_HALF:C_QUAD] = -0.5
    consts[:, C_QUAD:C_FOLD] = F * (rows[:, None] // 32 == np.arange(8)[None, :] // 2)
    consts[:, C_FOLD:C_END] = rows[:, None] % 32 == rows[None, :] % 32
    consts[:, C_EYE:C_EYE + P + E:E] = 1.0
    arrays = {
        "consts": consts,
        "patches": x,
        "tok_w": by_chunk(a["L0_tok_W"], KC),
        "w_qkv": np.stack([doubled(a[f"L0_attn_w_{n}"]) for n in "qkv"]),
        "w_o": by_chunk(a["L0_attn_w_o"], IC),
        "b_o": a["L0_attn_b_o"].reshape(1, D),
        "gate_w": doubled(a["L0_ffn_gate_w"]),
        "gate_b": a["L0_ffn_gate_b"].reshape(1, E),
        "fc1_w": np.stack([doubled(w) for w in a["L0_ffn_fc1_w"]]),
        "fc1_b": a["L0_ffn_fc1_b"].reshape(E, FC, P).transpose(0, 2, 1),
        "ln_w": a["L0_ffn_ln_w"].reshape(E, FC, P).transpose(2, 0, 1),
        "ln_b": a["L0_ffn_ln_b"].reshape(E, FC, P).transpose(2, 0, 1),
        "fc2_w": a["L0_ffn_fc2_w"].reshape(E, FC, P, D).transpose(0, 2, 1, 3),
        "fc2_b": np.concatenate([a["L0_ffn_fc2_b"]] * 8),
    }
    arrays = {k: np.ascontiguousarray(w) for k, w in arrays.items()}
    nc = bacc.Bacc("TRN2", target_bir_lowering=False, num_devices=1)
    ins = {k: nc.dram_tensor(f"in_{k}", w.shape, F32, kind="ExternalInput").ap() for k, w in arrays.items()}
    out = nc.dram_tensor("out_0", (IMAGES, SEQ, D), F32, kind="ExternalOutput").ap()
    vit_layer(nc, ins, out.rearrange("b n d -> (b n) d"))
    r = run_bass_kernel_spmd(nc, [{f"in_{k}": w for k, w in arrays.items()}], core_ids=[0])
    return r.results[0]["out_0"]
```
